# Optimizing a Trainium2 kernel written in Bass

```python
import numpy as np
import jax
import jax.numpy as jnp

def _softmax(x, axis=-1):
    return jax.nn.softmax(x, axis=axis)

def _gelu(x):
    return jax.nn.gelu(x, approximate=True)

def _silu(x):
    return jax.nn.silu(x)

def _sigmoid(x):
    return jax.nn.sigmoid(x)

def _layernorm(x, axis=-1, eps=1e-05):
    m = jnp.mean(x, axis=axis, keepdims=True)
    v = jnp.var(x, axis=axis, keepdims=True)
    return (x - m) / jnp.sqrt(v + eps)

def _scatter_add(tgt, idx, src, axis=0):
    return tgt.at[idx].add(src)

def _segment_sum(src, seg, n):
    return jax.ops.segment_sum(src, seg, n)
kernel_name = 'mk_adj_ffn_d1_adj_r2_9081e8'

def setup_inputs(seed: int=0):
    np.random.seed(seed)
    _w = jnp.asarray

    def _rec_inputs():
        import jax
        import jax.numpy as jnp
        _gk = jax.random.key(seed)
        x = -0.0002928 + 1 * jax.random.normal(jax.random.fold_in(_gk, 1), (32, 256, 128), jnp.float32)
        _a = jax.random.bernoulli(jax.random.fold_in(_gk, 2), 0.015625, (32, 256, 256))
        adj = _a.astype(jnp.int32)
        return (x, adj)
    x, adj = _rec_inputs()

    def _L0_gnn_setup():
        import jax, jax.numpy as jnp
        import numpy as np
        NEG_INF = -1000000000.0
        LEAKY_SLOPE = 0.2
        key = jax.random.key(seed)
        k1, k2, k3, k4 = jax.random.split(key, 4)
        B, N, D_in, D_out = (8, 1024, 128, 128)
        x = jax.random.normal(k1, (B, N, D_in), dtype=jnp.float32)
        adj_matrix = jax.random.randint(k2, (B, N, N), 0, 2, dtype=jnp.int32)
        W = jax.random.normal(k3, (D_out, D_in), dtype=jnp.float32) / np.sqrt(D_in)
        a = jax.random.normal(k4, (1, 2 * D_out), dtype=jnp.float32) / np.sqrt(2 * D_out)
        return {'x': x, 'adj_matrix': adj_matrix, 'W': W, 'a': a}
    _L0_gnn_all = _L0_gnn_setup()
    _L0_gnn_in = {k: v for k, v in _L0_gnn_all.items() if k in ('W', 'a')}
    del _L0_gnn_all

    def _L0_ffn_setup():
        import jax, jax.numpy as jnp
        import numpy as np
        TOP_K = 2
        key = jax.random.key(seed)
        ks = jax.random.split(key, 4)
        B, L, D, H, E = (8, 2048, 128, 512, 8)
        s = 0.02
        return {'x': jax.random.normal(ks[0], (B, L, D), jnp.float32), 'Wg': jax.random.normal(ks[1], (D, E), jnp.float32) * s, 'bg': jnp.zeros((E,), jnp.float32), 'W1': jax.random.normal(ks[2], (E, D, H), jnp.float32) * s, 'b1': jnp.zeros((E, H), jnp.float32), 'W2': jax.random.normal(ks[3], (E, H, D), jnp.float32) * s, 'b2': jnp.zeros((E, D), jnp.float32)}
    _L0_ffn_all = _L0_ffn_setup()
    _L0_ffn_in = {k: v for k, v in _L0_ffn_all.items() if k in ('Wg', 'bg', 'W1', 'b1', 'W2', 'b2')}
    del _L0_ffn_all
    return {'x': x, 'adj': adj, 'L0_gnn_W': _L0_gnn_in['W'], 'L0_gnn_a': _L0_gnn_in['a'], 'L0_ffn_Wg': _L0_ffn_in['Wg'], 'L0_ffn_bg': _L0_ffn_in['bg'], 'L0_ffn_W1': _L0_ffn_in['W1'], 'L0_ffn_b1': _L0_ffn_in['b1'], 'L0_ffn_W2': _L0_ffn_in['W2'], 'L0_ffn_b2': _L0_ffn_in['b2']}

def reference(x, adj, L0_gnn_W, L0_gnn_a, L0_ffn_Wg, L0_ffn_bg, L0_ffn_W1, L0_ffn_b1, L0_ffn_W2, L0_ffn_b2):
    import jax
    import jax.numpy as jnp

    def _L0_gnn_ref(x, adj_matrix, W, a):
        import jax, jax.numpy as jnp
        import numpy as np
        NEG_INF = -1000000000.0
        LEAKY_SLOPE = 0.2
        h = jnp.einsum('bnd,od->bno', x, W)
        D = h.shape[-1]
        a_left, a_right = (a[0, :D], a[0, D:])
        e = (h @ a_left)[:, :, None] + (h @ a_right)[:, None, :]
        e = jnp.where(e > 0, e, LEAKY_SLOPE * e)
        e = jnp.where(adj_matrix == 0, NEG_INF, e)
        alpha = jax.nn.softmax(e, axis=-1)
        return jnp.einsum('bij,bjd->bid', alpha, h)

    def _L0_ffn_ref(x, Wg, bg, W1, b1, W2, b2):
        import jax, jax.numpy as jnp
        import numpy as np
        TOP_K = 2
        B, L, D = x.shape
        E = W1.shape[0]
        xf = x.reshape(-1, D)
        gate_logits = xf @ Wg + bg
        top_w, top_i = jax.lax.top_k(gate_logits, TOP_K)
        top_w = jax.nn.softmax(top_w, axis=-1)
        w_dense = jnp.sum(jax.nn.one_hot(top_i, E, dtype=xf.dtype) * top_w[..., None], axis=1)
        out = jnp.zeros_like(xf)
        for e in range(E):
            h = jax.nn.gelu(xf @ W1[e] + b1[e], approximate=False)
            out = out + w_dense[:, e:e + 1] * (h @ W2[e] + b2[e])
        return out.reshape(B, L, D)
    x = x + _L0_gnn_ref(_layernorm(x, axis=-1), adj, L0_gnn_W, L0_gnn_a)
    x = x + _L0_ffn_ref(_layernorm(x, axis=-1), L0_ffn_Wg, L0_ffn_bg, L0_ffn_W1, L0_ffn_b1, L0_ffn_W2, L0_ffn_b2)
    return x

_drawn_inputs = setup_inputs


def setup_inputs(seed=0):
    import zlib

    import numpy as np

    out = dict(_drawn_inputs(seed))
    spreads = {'L0_ffn_bg': (0.0, 0.1), 'L0_ffn_b1': (0.0, 0.548), 'L0_ffn_b2': (0.0, 0.1)}
    factors = {}
    for name, (base, spread) in spreads.items():
        noise = np.random.default_rng([zlib.crc32(name.encode()), seed]).standard_normal(out[name].shape)
        drawn = base * np.exp(spread * noise) if base else spread * noise
        out[name] = jnp.asarray(drawn.astype(out[name].dtype))
    for name, factor in factors.items():
        out[name] = (out[name] * factor).astype(out[name].dtype)
    return out
```

```python
from contextlib import ExitStack

import concourse.bass as bass
from concourse import mybir

F32 = mybir.dt.float32
F16 = mybir.dt.float16
BF16 = mybir.dt.bfloat16
I32 = mybir.dt.int32
U32 = mybir.dt.uint32
ALU = mybir.AluOpType
ACT = mybir.ActivationFunctionType
AX = mybir.AxisListType.X
RMAX = bass.bass_isa.ReduceOp.max

P = 128
EPS = 1e-5
SLOPE = 0.2
MASKED = -1e30
REJECT = -3e38
X_SCALE = 1024.0
FAR = float(1 << 20)


def graph_moe(nc, x, adj, W, a, Wg, bg, W1, b1, W2, b2, out):
    B, N, D = x.shape
    E, _, H = W1.shape
    TOK = B * N
    TT = TOK // P
    GT = N // P
    G = 4
    BT = G * GT
    NB = B // G
    C = H // P
    T = 256
    TH = T // P
    NT = 2 * TOK // T + E
    NT += NT % 2
    SPARE = NT - 2 * TOK // T
    RS = TOK + T
    ROW = D + 2
    FC = 8
    FT = TT // FC
    assert D == P and GT == 2 and NT % 2 == 0 and (NT - 6) % 2 == 0

    x_v = x.rearrange("b (t p) d -> p (b t) d", p=P)
    out_v = out.rearrange("b (t p) d -> p (b t) d", p=P)
    adj_v = adj.rearrange("b (t p) j -> p (b t) j", p=P)
    rows_d = nc.dram_tensor("expert_rows", [E * RS + SPARE * T, ROW], F32).ap()
    y_d = nc.dram_tensor("expert_out", [2 * TOK, D], F32).ap()
    y_v = y_d.rearrange("(k t p) d -> p k t d", k=2, p=P)

    with ExitStack() as ctx:
        def sb(name, shape, dt=F32):
            return ctx.enter_context(nc.sbuf_tensor(name, shape, dt))

        def sem(name):
            return ctx.enter_context(nc.semaphore(name))

        bank = [ctx.enter_context(nc.psum_tensor(f"bank{i}", [P, 512], F32)) for i in range(8)]

        ident = sb("ident", [P, P])
        ident16 = sb("ident16", [P, P], F16)
        ones = sb("ones", [P, P])
        ones16 = sb("ones16", [P, P], BF16)
        before = sb("before", [P, P])
        before16 = sb("before16", [P, P], BF16)
        ramp = sb("ramp", [P, BT, E])
        region = sb("region", [P, BT, E])
        token_id = sb("token_id", [P, TT])
        tau = sb("tau", [P, NT])
        filler = sb("filler", [P, SPARE * TH, ROW])
        w_in = sb("w_in", [P, D])
        wT = sb("wT", [P, D])
        wa = sb("wa", [P, 2])
        wr_rep = sb("wr_rep", [P, P])
        wg = sb("wg", [P, E])
        bg_rep = sb("bg_rep", [P, E])
        b1_in = sb("b1_in", [E * C + 2, P])
        b1T = sb("b1T", [P, E * C + 2])
        b2_rep = sb("b2_rep", [P, E * D])
        w1f = sb("w1f", [P, E * H])
        w2f = sb("w2f", [P, E * H])
        w1h = sb("w1h", [P, E * H], F16)
        w1l = sb("w1l", [P, E * H], F16)
        w2h = sb("w2h", [P, E * H], F16)
        w2l = sb("w2l", [P, E * H], F16)
        wmax = sb("wmax", [P, 4])
        wmax_all = sb("wmax_all", [P, 4])
        pow2 = sb("pow2", [P, 4], I32)
        scale = sb("scale", [P, 4])
        inv = sb("inv", [P, 4])
        X = sb("X", [P, TT, D])
        adj_sb = sb("adj_sb", [P, BT, N], I32)
        S = sb("S", [P, BT, N])
        xn = sb("xn", [P, BT, D])
        xn2 = sb("xn2", [P, BT, D])
        stats = sb("stats", [P, BT, 6])
        mv = sb("mv", [P, BT, 2])
        rstd = sb("rstd", [P, BT])
        newton = sb("newton", [P, BT])
        xnT = sb("xnT", [P, G, N])
        h_sb = sb("h_sb", [P, G, N])
        pT = sb("pT", [P, G, 2 * N])
        left = sb("left", [P, BT])
        rmax = sb("rmax", [P, BT])
        nsum = sb("nsum", [P, BT])
        negm = sb("negm", [P, BT])
        psum_p = sb("psum_p", [P, BT])
        rsum = sb("rsum", [P, BT])
        pack = sb("pack", [P, BT, ROW])
        lg = sb("lg", [P, BT, E])
        tmp = sb("tmp", [P, BT, E])
        oh1 = sb("oh1", [P, BT, E])
        oh2 = sb("oh2", [P, BT, E])
        picks = sb("picks", [P, BT, E], BF16)
        picks_before = sb("picks_before", [P, E])
        picks_sum = sb("picks_sum", [P, E])
        picks_before16 = sb("picks_before16", [P, E], BF16)
        m1 = sb("m1", [P, BT])
        m2 = sb("m2", [P, BT])
        f1 = sb("f1", [P, BT])
        f2 = sb("f2", [P, BT])
        slot = sb("slot", [P, BT, E])
        target_f = sb("target_f", [P, 2, BT])
        target = sb("target", [P, 2, BT], U32)
        gap = sb("gap", [P, TT])
        wts = sb("wts", [P, 2, TT])
        cnt = sb("cnt", [P, E])
        cnt_i = sb("cnt_i", [P, E], I32)
        tiles = sb("tiles", [P, E])
        cum = sb("cum", [P, 4, E])
        done = sb("done", [P, NT, E])
        donec = sb("donec", [P, NT, E])
        tab_e = sb("tab_e", [P, NT])
        tab_k = sb("tab_k", [P, NT])
        tab_row = sb("tab_row", [P, NT])
        tab_f = sb("tab_f", [P, NT])
        expert_of = sb("expert_of", [P, NT], I32)
        row_of = sb("row_of", [P, NT], I32)
        fill_row = sb("fill_row", [P, E], I32)
        XL = sb("XL", [P, 2, TH, ROW])
        xT = sb("xT", [P, 2, 2 * T], F16)
        hid = sb("hid", [P, 2, C * T])
        hh = sb("hh", [P, 2, C * T], F16)
        hl = sb("hl", [P, 2, C * T], F16)
        y_sb = sb("y_sb", [P, 2, T])
        back = sb("back", [P, NT, TH])
        back_u = sb("back_u", [P, 2, TH], U32)
        yf = sb("yf", [P, 2, 2, FT, D])

        s_const = sem("s_const")
        s_wl = sem("s_wl")
        s_ew = sem("s_ew")
        s_filled = sem("s_filled")
        s_x = sem("s_x")
        s_adj = sem("s_adj")
        s_cast = sem("s_cast")
        s_prep_ps = sem("s_prep_ps")
        s_prep = sem("s_prep")
        s_amax = sem("s_amax")
        s_gmax = sem("s_gmax")
        s_scale = sem("s_scale")
        s_whi = sem("s_whi")
        s_wlo = sem("s_wlo")
        s_mask = sem("s_mask")
        s_xn = sem("s_xn")
        s_t = sem("s_t")
        s_ts = sem("s_ts")
        s_hr = sem("s_hr")
        s_h = sem("s_h")
        s_s = sem("s_s")
        s_negm = sem("s_negm")
        s_sum = sem("s_sum")
        s_leaky = sem("s_leaky")
        s_p = sem("s_p")
        s_pt = sem("s_pt")
        s_pts = sem("s_pts")
        s_av = sem("s_av")
        s_x1 = sem("s_x1")
        s_xn2 = sem("s_xn2")
        s_lg = sem("s_lg")
        s_picks = sem("s_picks")
        s_rank = sem("s_rank")
        s_pack = sem("s_pack")
        s_turn = sem("s_turn")
        s_scat = sem("s_scat")
        s_packfree = sem("s_packfree")
        s_gap = sem("s_gap")
        s_egap = sem("s_egap")
        s_cnt = sem("s_cnt")
        s_tab = sem("s_tab")
        s_load = [sem(f"s_load{i}") for i in range(2)]
        s_tt = sem("s_tt")
        s_tts = sem("s_tts")
        s_z = sem("s_z")
        s_g = sem("s_g")
        s_split = sem("s_split")
        s_y = sem("s_y")
        s_back = sem("s_back")
        s_ys = sem("s_ys")
        s_ysc = [sem(f"s_ysc{i}") for i in range(2)]
        s_yl = [sem(f"s_yl{i}") for i in range(2)]
        s_fin = sem("s_fin")
        s_out = sem("s_out")
        s_vturn = sem("s_vturn")
        s_sturn = sem("s_sturn")
        s_v = sem("s_v")
        s_vb = sem("s_vb")
        s_vt = sem("s_vt")
        s_ve = sem("s_ve")
        s_vf = sem("s_vf")

        T_BANK = bank[0]
        HR = [bank[1], bank[2]]
        PT = [bank[3], bank[4]]
        AV = [bank[5], bank[6]]
        MISC = bank[7]
        LEFT = MISC[:, 0:BT]
        LOGITS = MISC[:, 64:64 + BT * E]
        RANK = MISC[:, 128:128 + BT * E]
        COUNT = MISC[:, 192:192 + E]
        TB = [bank[0], bank[7]]
        Z = [[bank[1], bank[2]], [bank[3], bank[4]]]
        Y = [bank[5], bank[6]]

        block = ctx.enter_context(nc.Block())

        @block.sync
        def _(sp):
            for dst, src in ((w_in[:, :], W), (wg[:, :], Wg),
                             (b1_in[0:E * C, :], b1.rearrange("e (c p) -> (e c) p", p=P))):
                sp.dma_start(dst, src).then_inc(s_wl, 16)
            with sp.Fori(0, NB) as b:
                sp.wait_ge(s_mask, b + 1)
                sp.dma_start(X[:, bass.ds(b * BT, BT), :], x_v[:, bass.ds(b * BT, BT), :]).then_inc(s_x, 16)
                sp.dma_start(adj_sb[:, :, :], adj_v[:, bass.ds(b * BT, BT), :]).then_inc(s_adj, 16)
                sp.wait_ge(s_x, b * 16 + 16)
                sp.wait_ge(s_adj, b * 16 + 16)
                sp.sem_inc(s_sturn, 1)
            sp.wait_ge(s_tab, 1)
            for e in range(E):
                row = sp.value_load(fill_row[0:1, e:e + 1], min_val=0, max_val=E * RS)
                sp.dma_start(rows_d[bass.ds(row, T), :].rearrange("(h p) r -> p h r", p=P),
                             filler[:, 0:TH, :]).then_inc(s_filled, 16)
            sp.wait_ge(s_filled, 16 * (E + 1))
            sp.wait_ge(s_scat, 16 * 2 * BT * NB)

            def load(s, k, wait):
                if wait:
                    sp.wait_ge(s_tt, s - 1)
                    sp.wait_ge(s_back, s - 1)
                    sp.sem_inc(s_sturn, 1)
                row = sp.value_load(row_of[0:1, bass.ds(s, 1)], min_val=0, max_val=E * RS + SPARE * T - T)
                sp.dma_start(XL[:, k, :, :], rows_d[bass.ds(row, T), :].rearrange("(h p) r -> p h r", p=P)
                             ).then_inc(s_load[k], 16)

            load(0, 0, False)
            load(1, 1, False)
            with sp.Fori(1, NT // 2) as r:
                for k in range(2):
                    load(r * 2 + k, k, True)
            for k in range(2):
                sp.wait_ge(s_ysc[k], 16 * TH * NT // 2)

            def load_y(q, k):
                for c in range(2):
                    sp.dma_start(yf[:, k, c, :, :], y_v[:, c, bass.ds(q * FT, FT), :]).then_inc(s_yl[k], 16)

            load_y(0, 0)
            load_y(1, 1)
            with sp.Fori(1, FC // 2) as r:
                for k in range(2):
                    sp.wait_ge(s_fin, r * 2 + (k - 1))
                    load_y(r * 2 + k, k)

        @block.gpsimd
        def _(pool):
            pool.memset(ident[:, :], 0.0)
            pool.memset(ones[:, :], 1.0)
            pool.memset(picks_before[:, :], 0.0)
            pool.memset(filler[:, :, 0:D + 1], 0.0)
            pool.memset(filler[:, :, D + 1:ROW], 0.0).then_inc(s_const, 1)
            pool.wait_ge(s_const, 1)
            pool.memset(filler[:, :, D:D + 1], FAR)
            pool.affine_select(out=ident[:, :], in_=ident[:, :], compare_op=ALU.not_equal, fill=1.0, base=0,
                               pattern=[[-1, P]], channel_multiplier=1)
            pool.affine_select(out=before[:, :], in_=ones[:, :], compare_op=ALU.is_gt, fill=0.0, base=0,
                               pattern=[[1, P]], channel_multiplier=-1)
            pool.iota(ramp[:, :, :], pattern=[[0, BT], [-1, E]], base=E, channel_multiplier=0,
                      allow_small_or_imprecise_dtypes=True)
            pool.iota(region[:, :, :], pattern=[[0, BT], [RS, E]], base=0, channel_multiplier=0,
                      allow_small_or_imprecise_dtypes=True)
            pool.iota(token_id[:, :], pattern=[[P, TT]], base=0, channel_multiplier=1,
                      allow_small_or_imprecise_dtypes=True)
            pool.iota(tau[:, :], pattern=[[1, NT]], base=0, channel_multiplier=0,
                      allow_small_or_imprecise_dtypes=True).then_inc(s_const, 1)
            pool.wait_ge(s_amax, 1)
            pool.partition_all_reduce(wmax_all[:, :], wmax[:, :], P, RMAX).then_inc(s_gmax, 1)
            for n, (full, hi, lo) in enumerate(((w1f, w1h, w1l), (w2f, w2h, w2l))):
                pool.wait_ge(s_whi, n + 1)
                pool.tensor_scalar(full[:, :], full[:, :], scale[:, n:n + 1], None, ALU.mult).then_inc(s_wlo, 1)
                pool.wait_ge(s_wlo, 2 * n + 1)
                pool.tensor_tensor(lo[:, :], full[:, :], hi[:, :], ALU.subtract).then_inc(s_wlo, 1)
            with pool.Fori(0, NB) as b:
                pool.wait_ge(s_pack, b + 1)
                pool.sem_inc(s_turn, 1)
                for c in range(2):
                    for t in range(BT):
                        pool.indirect_dma_start(
                            rows_d[:, :], bass.IndirectOffsetOnAxis(ap=target[:, c, t:t + 1], axis=0),
                            pack[:, t, :], None).then_inc(s_scat, 16)
                pool.wait_ge(s_scat, b * (16 * 2 * BT) + 16 * 2 * BT)
                pool.sem_inc(s_packfree, 1)
            with pool.Fori(0, NT // 2) as r:
                for k in range(2):
                    pool.wait_ge(s_ys, r * 2 + (k + 1))
                    pool.sem_inc(s_turn, 1)
                    for half in range(TH):
                        pool.indirect_dma_start(
                            y_d[:, :], bass.IndirectOffsetOnAxis(ap=back_u[:, k, half:half + 1], axis=0),
                            y_sb[:, k, half * P:(half + 1) * P], None,
                            bounds_check=2 * TOK - 1, oob_is_err=False).then_inc(s_ysc[k], 16)

        @block.scalar
        def _(act):
            act.dma_start(b1_in[E * C:, :], a.rearrange("o (s p) -> (o s) p", p=P)).then_inc(s_wl, 16)
            act.dma_start(bg_rep[:, :], bg.rearrange("(o e) -> o e", o=1).broadcast_to([P, E])).then_inc(s_wl, 16)
            act.dma_start(b2_rep[:, :], b2.rearrange("(o e) d -> o (e d)", o=1).broadcast_to([P, E * D])
                          ).then_inc(s_wl, 16)
            act.dma_start(w1f[:, :].rearrange("p (e h) -> p e h", e=E), W1.rearrange("e d h -> d e h")
                          ).then_inc(s_ew, 16)
            act.dma_start(w2f[:, :].rearrange("p (k d) -> p k d", d=D), W2.rearrange("e (c p) d -> p (e c) d", p=P)
                          ).then_inc(s_ew, 16)
            act.wait_ge(s_const, 2)
            act.dma_start(rows_d[E * RS:E * RS + SPARE * T, :].rearrange("(h p) r -> p h r", p=P),
                          filler[:, :, :]).then_inc(s_filled, 16)
            act.wait_ge(s_scale, 1)
            for n, (full, hi) in enumerate(((w1f, w1h), (w2f, w2h))):
                act.activation(hi[:, :], full[:, :], ACT.Copy, scale=scale[:, n:n + 1]).then_inc(s_whi, 1)

            with act.Fori(0, NB) as b:
                def turned(i, g):
                    act.wait_ge(s_t, b * (2 * G) + (i * G + g + 1))
                    act.activation(xnT[:, g, :], T_BANK[:, 0:N], ACT.Copy).then_inc(s_ts, 1)

                def add_left(g):
                    for t in range(g * GT, (g + 1) * GT):
                        last = act.activation(S[:, t, :], S[:, t, :], ACT.Identity, bias=left[:, t:t + 1])
                    last.then_inc(s_sum, 1)

                def probs(g):
                    act.wait_ge(s_leaky, b * G + (g + 1))
                    for t in range(g * GT, (g + 1) * GT):
                        last = act.activation(S[:, t, :], S[:, t, :], ACT.Exp, bias=negm[:, t:t + 1],
                                              accum_out=psum_p[:, t:t + 1])
                    last.then_inc(s_p, 1)

                for g in range(G):
                    turned(0, g)
                    act.wait_ge(s_hr, b * G + (g + 1))
                    act.activation(h_sb[:, g, :], HR[g % 2][:, 0:N], ACT.Copy).then_inc(s_h, 1)
                act.wait_ge(s_negm, b + 1)
                for g in range(G + 1):
                    if g < G:
                        add_left(g)
                    if g >= 1:
                        probs(g - 1)
                for g in range(G):
                    turned(1, g)
            act.wait_ge(s_gap, 1)
            act.activation(gap[:, :], gap[:, :], ACT.Exp).then_inc(s_egap, 1)

            act.wait_ge(s_tab, 1)

            def turned_tile(s, k):
                act.wait_ge(s_tt, s + 1)
                act.activation(xT[:, k, :], TB[k][:, 0:T].bitcast(F16), ACT.Copy).then_inc(s_tts, 1)

            def gelu(s, k, wait):
                e = act.value_load(expert_of[0:1, bass.ds(s, 1)], min_val=0, max_val=E - 1)
                for c in range(C):
                    if c % 2 == 0:
                        act.wait_ge(s_z, s * 2 + (c // 2 + 1))
                        if wait:
                            act.wait_ge(s_split, s * 2 + (c // 2 - 3))
                    ins = act.activation(hid[:, k, c * T:(c + 1) * T], Z[k][c // 2][:, (c % 2) * T:(c % 2 + 1) * T],
                                         ACT.Gelu, bias=b1T[:, bass.ds(e * C + c, 1)], scale=inv[:, 0:1])
                    if c % 2 == 1:
                        ins.then_inc(s_g, 1)

            turned_tile(0, 0)
            for s in range(2):
                turned_tile(s + 1, (s + 1) % 2)
                gelu(s, s % 2, False)
            with act.Fori(1, NT // 2 - 1) as r:
                for k in range(2):
                    turned_tile(r * 2 + (k + 1), (k + 1) % 2)
                    gelu(r * 2 + k, k, True)
            turned_tile(NT - 1, 1)
            gelu(NT - 2, 0, True)
            gelu(NT - 1, 1, True)

            with act.Fori(0, FC) as q:
                act.wait_ge(s_fin, q + 1)
                act.dma_start(out_v[:, bass.ds(q * FT, FT), :], X[:, bass.ds(q * FT, FT), :]).then_inc(s_out, 16)
            act.wait_ge(s_out, 16 * FC)

        @block.tensor
        def _(pe):
            pe.wait_ge(s_const, 2)
            pe.wait_ge(s_wl, 16 * 6)
            pe.transpose(T_BANK[:, 0:D], w_in[:, :], ident[:, :])
            pe.transpose(T_BANK[:, 256:256 + E * C + 2], b1_in[:, :], ident[0:E * C + 2, 0:E * C + 2]
                         ).then_inc(s_prep_ps, 1)
            pe.wait_ge(s_prep, 1)
            pe.matmul(T_BANK[:, 128:130], w_in[:, :], b1T[:, E * C:], start=True, stop=True).then_inc(s_prep_ps, 1)
            pe.wait_ge(s_prep, 2)

            with pe.Fori(0, NB) as b:
                def turn(i, g, src):
                    if i or g:
                        pe.wait_ge(s_ts, b * (2 * G) + (i * G + g))
                    for t in range(GT):
                        last = pe.transpose(T_BANK[:, t * P:(t + 1) * P], src[:, g * GT + t, :], ident[:, :])
                    last.then_inc(s_t, 1)

                def project(g):
                    hr = HR[g % 2]
                    pe.wait_ge(s_ts, b * (2 * G) + (g + 1))
                    if g >= 2:
                        pe.wait_ge(s_s, b * G + (g - 1))
                        pe.wait_ge(s_h, b * G + (g - 1))
                    for t in range(GT):
                        pe.matmul(hr[:, t * P:(t + 1) * P], xnT[:, g, t * P:(t + 1) * P], wT[:, :],
                                  start=True, stop=True)
                    for t in range(GT):
                        pe.matmul(LEFT[:, g * GT + t:g * GT + t + 1], xnT[:, g, t * P:(t + 1) * P], wa[:, 0:1],
                                  start=True, stop=True)
                    pe.matmul(hr[:, N:2 * N], wr_rep[:, :], xnT[:, g, :], start=True, stop=True).then_inc(s_hr, 1)

                def turn_probs(g):
                    pe.wait_ge(s_p, b * G + (g + 1))
                    if g >= 2:
                        pe.wait_ge(s_pts, b * G + (g - 1))
                    for j in range(GT):
                        for t in range(GT):
                            last = pe.transpose(PT[g % 2][:, j * N + t * P:j * N + (t + 1) * P],
                                                S[:, g * GT + t, j * P:(j + 1) * P], ident[:, :])
                    last.then_inc(s_pt, 1)

                def attend(g):
                    pe.wait_ge(s_pts, b * G + (g + 1))
                    if g >= 2:
                        pe.wait_ge(s_x1, b * G + (g - 1))
                    for t in range(GT):
                        for j in range(GT):
                            last = pe.matmul(AV[g % 2][:, t * P:(t + 1) * P],
                                             pT[:, g, j * N + t * P:j * N + (t + 1) * P],
                                             h_sb[:, g, j * P:(j + 1) * P], start=(j == 0), stop=(j == GT - 1))
                    last.then_inc(s_av, 1)

                def route(g):
                    pe.wait_ge(s_ts, b * (2 * G) + (G + g + 1))
                    for t in range(GT):
                        n = (g * GT + t) * E
                        last = pe.matmul(LOGITS[:, n:n + E], xnT[:, g, t * P:(t + 1) * P], wg[:, :],
                                         start=True, stop=True)
                    if g == G - 1:
                        last.then_inc(s_lg, 1)

                for g in range(G):
                    pe.wait_ge(s_xn, b * G + (g + 1))
                    turn(0, g, xn)
                    project(g)
                for g in range(G + 1):
                    if g < G:
                        turn_probs(g)
                    if g >= 1:
                        attend(g - 1)
                for g in range(G):
                    pe.wait_ge(s_xn2, b * G + (g + 1))
                    turn(1, g, xn2)
                    route(g)
                pe.wait_ge(s_picks, b + 1)
                flat = picks[:, :, :].rearrange("p t e -> p (t e)")
                pe.matmul(RANK[:, :], before16[:, :], flat, start=True, stop=False)
                for t in range(1, BT):
                    pe.matmul(RANK[:, t * E:], ones16[:, :], flat[:, 0:(BT - t) * E], start=False, stop=False)
                pe.matmul(RANK[:, :].rearrange("p (t e) -> p t e", e=E), ones16[:, :],
                          picks_before16[:, :].rearrange("p (o e) -> p o e", o=1).broadcast_to([P, BT, E]),
                          start=False, stop=True).then_inc(s_rank, 1)
            pe.wait_ge(s_pack, NB)
            pe.matmul(COUNT, ones16[:, :], picks_before16[:, :], start=True, stop=True).then_inc(s_cnt, 1)

            pe.wait_ge(s_tab, 1)
            pe.wait_ge(s_wlo, 4)

            def turn_tile(s, k, round_):
                pe.wait_ge(s_load[k], round_ * 16 + 16)
                parts = XL[:, k, :, :].bitcast(F16)
                tb = TB[k][:, 0:T].bitcast(F16)
                for part in range(2):
                    for half in range(TH):
                        last = pe.transpose(tb[:, part * T + half * P:part * T + (half + 1) * P],
                                            parts[:, half, part * D:(part + 1) * D], ident16[:, :])
                last.then_inc(s_tt, 1)

            def hidden(s, k, wait):
                e = pe.value_load(expert_of[0:1, bass.ds(s, 1)], min_val=0, max_val=E - 1)
                pe.wait_ge(s_tts, s + 1)
                for c in range(C):
                    if wait and c % 2 == 0:
                        pe.wait_ge(s_g, s * 2 + (c // 2 - 3))
                    z = Z[k][c // 2][:, (c % 2) * T:(c % 2 + 1) * T]
                    hi = w1h[:, bass.ds(e * H + c * P, P)]
                    lo = w1l[:, bass.ds(e * H + c * P, P)]
                    pe.matmul(z, hi, xT[:, k, 0:T], start=True, stop=False)
                    pe.matmul(z, hi, xT[:, k, T:2 * T], start=False, stop=False)
                    last = pe.matmul(z, lo, xT[:, k, 0:T], start=False, stop=True)
                    if c % 2 == 1:
                        last.then_inc(s_z, 1)

            def output(u, k, wait):
                e = pe.value_load(expert_of[0:1, bass.ds(u, 1)], min_val=0, max_val=E - 1)
                pe.wait_ge(s_split, u * 2 + 2)
                if wait:
                    pe.wait_ge(s_ys, u - 1)
                for half in range(TH):
                    y = Y[k][:, half * P:(half + 1) * P]
                    for c in range(C):
                        at = slice(c * T + half * P, c * T + (half + 1) * P)
                        hi = w2h[:, bass.ds(e * H + c * P, P)]
                        lo = w2l[:, bass.ds(e * H + c * P, P)]
                        pe.matmul(y, hh[:, k, at], hi, start=(c == 0), stop=False)
                        pe.matmul(y, hh[:, k, at], lo, start=False, stop=False)
                        last = pe.matmul(y, hl[:, k, at], hi, start=False, stop=(c == C - 1))
                last.then_inc(s_y, 1)

            turn_tile(0, 0, 0)
            for s in range(4):
                if s >= 2:
                    output(s - 2, s % 2, False)
                turn_tile(s + 1, (s + 1) % 2, (s + 1) // 2)
                hidden(s, s % 2, s >= 2)
            with pe.Fori(2, NT // 2 - 1) as r:
                for k in range(2):
                    output(r * 2 + (k - 2), k, True)
                    turn_tile(r * 2 + (k + 1), (k + 1) % 2, r + k)
                    hidden(r * 2 + k, k, True)
            for s in range(NT - 2, NT + 2):
                output(s - 2, s % 2, True)
                if s == NT - 2:
                    turn_tile(s + 1, 1, NT // 2 - 1)
                if s < NT:
                    hidden(s, s % 2, True)

        @block.vector
        def _(dve):
            count = [0]

            def link(ins, sem_, base=0):
                count[0] += 1
                ins.then_inc(sem_, 1)
                dve.wait_ge(sem_, base + count[0])

            dve.sem_inc(s_mask, 1)
            dve.sem_inc(s_packfree, 1)
            dve.wait_ge(s_const, 2)
            dve.tensor_copy(ident16[:, :], ident[:, :])
            dve.tensor_copy(ones16[:, :], ones[:, :])
            dve.tensor_copy(before16[:, :], before[:, :])
            dve.memset(picks_before16[:, :], 0.0)
            dve.wait_ge(s_prep_ps, 1)
            dve.tensor_copy(wT[:, :], T_BANK[:, 0:D])
            dve.tensor_copy(b1T[:, :], T_BANK[:, 256:256 + E * C + 2]).then_inc(s_prep, 1)
            dve.wait_ge(s_prep_ps, 2)
            link(dve.tensor_copy(wa[:, :], T_BANK[:, 128:130]), s_v)
            dve.tensor_scalar(wr_rep[:, :], ones[:, :], wa[:, 1:2], None, ALU.mult).then_inc(s_prep, 1)
            dve.wait_ge(s_ew, 32)
            dve.tensor_reduce(wmax[:, 0:1], w1f[:, :], AX, ALU.max, apply_absolute_value=True)
            dve.tensor_reduce(wmax[:, 1:2], w2f[:, :], AX, ALU.max, apply_absolute_value=True)
            link(dve.tensor_reduce(wmax[:, 2:3], b1T[:, 0:E * C], AX, ALU.max, apply_absolute_value=True), s_v)
            dve.tensor_copy(wmax[:, 3:4], wmax[:, 2:3]).then_inc(s_amax, 1)
            dve.wait_ge(s_gmax, 1)
            link(dve.scalar_tensor_tensor(wmax_all[:, 2:3], wmax_all[:, 0:1], float(D), wmax_all[:, 2:3],
                                          ALU.mult, ALU.add), s_v)
            link(dve.tensor_scalar(wmax_all[:, :], wmax_all[:, :], 1e-12, None, ALU.max), s_v)
            link(dve.tensor_scalar(pow2[:, :], wmax_all[:, :].bitcast(I32), 0x7F800000, None, ALU.bitwise_and), s_v)
            link(dve.tensor_scalar(scale[:, :].bitcast(I32), pow2[:, :], -1.0, float((254 + 13) << 23),
                                   ALU.mult, ALU.add), s_v)
            link(dve.tensor_scalar(inv[:, :].bitcast(I32), scale[:, :].bitcast(I32), -1.0, float(254 << 23),
                                   ALU.mult, ALU.add), s_v)
            dve.tensor_tensor(inv[:, 1:2], inv[:, 1:2], inv[:, 2:3], ALU.mult)
            dve.tensor_scalar(inv[:, 0:1], inv[:, 0:1], 1.0 / X_SCALE, None, ALU.mult).then_inc(s_scale, 1)

            count[0] = 0
            LINKS = 51
            with dve.Fori(0, NB) as b:
                base = b * LINKS
                tile0 = b * BT

                def lk(ins):
                    link(ins, s_vb, base)

                def layernorm(dst, done_sem):
                    for t in range(BT):
                        last = dve.bn_stats(stats[:, t, :], X[:, bass.ds(tile0 + t, 1), :])
                    lk(last)
                    dve.sem_inc(s_vturn, 1)
                    for t in range(BT):
                        last = dve.bn_aggr(mv[:, t, :], stats[:, t, :])
                    lk(last)
                    lk(dve.tensor_scalar(mv[:, :, 1], mv[:, :, 1], EPS, float(1 << 26), ALU.add, ALU.mult))
                    lk(dve.tensor_scalar(rstd[:, :].bitcast(I32), mv[:, :, 1].bitcast(I32), 1, None,
                                         ALU.logical_shift_right))
                    lk(dve.tensor_scalar(rstd[:, :].bitcast(I32), rstd[:, :].bitcast(I32), -1.0,
                                         float(0x5F3759DF), ALU.mult, ALU.add))
                    for grown in (1.0, 2.0, 16.0):
                        lk(dve.tensor_tensor(newton[:, :], rstd[:, :], mv[:, :, 1], ALU.mult))
                        lk(dve.tensor_tensor(newton[:, :], newton[:, :], rstd[:, :], ALU.mult))
                        lk(dve.scalar_tensor_tensor(rstd[:, :], newton[:, :], 3.0 * grown * grown, rstd[:, :],
                                                    ALU.subtract, ALU.mult, reverse0=True))
                    for t in range(BT):
                        last = dve.tensor_scalar(dst[:, t, :], X[:, bass.ds(tile0 + t, 1), :], mv[:, t, 0:1],
                                                 rstd[:, t:t + 1], ALU.subtract, ALU.mult)
                        if t % GT == GT - 1:
                            last.then_inc(done_sem, 1)

                dve.wait_ge(s_x, b * 16 + 16)
                dve.sem_inc(s_vturn, 1)
                layernorm(xn, s_xn)
                dve.wait_ge(s_adj, b * 16 + 16)
                dve.tensor_scalar(S[:, :, :], adj_sb[:, :, :], 0.0, MASKED, ALU.is_equal, ALU.mult
                                  ).then_inc(s_mask, 1)
                dve.wait_ge(s_mask, b + 2)
                for g in range(G):
                    dve.wait_ge(s_h, b * G + (g + 1))
                    dve.sem_inc(s_vturn, 1)
                    for t in range(g * GT, (g + 1) * GT):
                        last = dve.tensor_tensor_reduce(S[:, t, :], S[:, t, :], HR[g % 2][:, N:2 * N], 1.0, -3e38,
                                                        ALU.add, ALU.max, rmax[:, t:t + 1])
                    last.then_inc(s_s, 1)
                lk(dve.tensor_copy(left[:, :], LEFT))
                dve.wait_ge(s_s, b * G + G)
                lk(dve.scalar_tensor_tensor(nsum[:, :], rmax[:, :], -1.0, left[:, :], ALU.mult, ALU.subtract))
                lk(dve.scalar_tensor_tensor(negm[:, :], nsum[:, :], SLOPE, nsum[:, :], ALU.mult, ALU.min))
                dve.tensor_copy(nsum[:, :], negm[:, :]).then_inc(s_negm, 1)
                for g in range(G):
                    dve.wait_ge(s_sum, b * G + (g + 1))
                    both = S[:, g * GT:(g + 1) * GT, :]
                    dve.scalar_tensor_tensor(both, both, SLOPE, both, ALU.mult, ALU.max).then_inc(s_leaky, 1)
                for g in range(G):
                    dve.wait_ge(s_pt, b * G + (g + 1))
                    dve.tensor_copy(pT[:, g, :], PT[g % 2][:, :]).then_inc(s_pts, 1)
                dve.wait_ge(s_p, b * G + G)
                lk(dve.reciprocal(rsum[:, :], psum_p[:, :]))
                for g in range(G):
                    dve.wait_ge(s_av, b * G + (g + 1))
                    for t in range(g * GT, (g + 1) * GT):
                        xt = X[:, bass.ds(tile0 + t, 1), :].rearrange("p o d -> p (o d)")
                        last = dve.scalar_tensor_tensor(xt, AV[g % 2][:, (t % GT) * P:(t % GT + 1) * P],
                                                        rsum[:, t:t + 1], xt, ALU.mult, ALU.add)
                    last.then_inc(s_x1, 1)
                dve.wait_ge(s_x1, b * G + G)
                dve.sem_inc(s_vturn, 1)
                layernorm(xn2, s_xn2)
                dve.wait_ge(s_xn2, b * G + G)

                dve.wait_ge(s_packfree, b + 1)
                hi = pack[:, :, 0:D // 2].bitcast(F16)
                lo = pack[:, :, D // 2:D].bitcast(F16)
                lk(dve.tensor_scalar(hi, xn2[:, :, :], X_SCALE, None, ALU.mult))
                dve.scalar_tensor_tensor(lo, xn2[:, :, :], X_SCALE, hi, ALU.mult, ALU.subtract)
                dve.tensor_copy(pack[:, :, D], token_id[:, bass.ds(tile0, BT)])

                def over_e(v):
                    return v[:, :].rearrange("p (t o) -> p t o", o=1).broadcast_to([P, BT, E])

                def choose(oh, m, f):
                    lk(dve.tensor_reduce(m[:, :], lg[:, :, :], AX, ALU.max))
                    lk(dve.tensor_tensor(tmp[:, :, :], lg[:, :, :], over_e(m), ALU.is_equal))
                    lk(dve.tensor_tensor(tmp[:, :, :], tmp[:, :, :], ramp[:, :, :], ALU.mult))
                    lk(dve.tensor_reduce(f[:, :], tmp[:, :, :], AX, ALU.max))
                    lk(dve.tensor_tensor(oh[:, :, :], ramp[:, :, :], over_e(f), ALU.is_equal))

                dve.wait_ge(s_lg, b + 1)
                lk(dve.tensor_tensor(lg[:, :, :], LOGITS.rearrange("p (t e) -> p t e", e=E),
                                     bg_rep[:, :].rearrange("p (o e) -> p o e", o=1).broadcast_to([P, BT, E]),
                                     ALU.add))
                choose(oh1, m1, f1)
                lk(dve.scalar_tensor_tensor(lg[:, :, :], oh1[:, :, :], REJECT, lg[:, :, :], ALU.mult, ALU.add))
                choose(oh2, m2, f2)
                dve.tensor_tensor(picks[:, :, :], oh1[:, :, :], oh2[:, :, :], ALU.add).then_inc(s_picks, 1)
                dve.tensor_copy(pack[:, :, D + 1], f2[:, :])
                dve.tensor_tensor(gap[:, bass.ds(tile0, BT)], m2[:, :], m1[:, :], ALU.subtract)
                dve.wait_ge(s_picks, b + 1)
                lk(dve.tensor_reduce(picks_sum[:, :], picks[:, :, :].rearrange("p t e -> p e t"), AX, ALU.add))
                lk(dve.tensor_tensor(picks_before[:, :], picks_before[:, :], picks_sum[:, :], ALU.add))
                dve.wait_ge(s_rank, b + 1)
                dve.tensor_copy(picks_before16[:, :], picks_before[:, :])
                lk(dve.tensor_tensor(slot[:, :, :], RANK.rearrange("p (t e) -> p t e", e=E), region[:, :, :],
                                     ALU.add))
                lk(dve.tensor_tensor(oh1[:, :, :], oh1[:, :, :], slot[:, :, :], ALU.mult))
                dve.tensor_reduce(target_f[:, 0, :], oh1[:, :, :], AX, ALU.add)
                lk(dve.tensor_tensor(oh2[:, :, :], oh2[:, :, :], slot[:, :, :], ALU.mult))
                lk(dve.tensor_reduce(target_f[:, 1, :], oh2[:, :, :], AX, ALU.add))
                dve.tensor_copy(target[:, :, :], target_f[:, :, :]).then_inc(s_pack, 1)
                assert count[0] == LINKS, count[0]

            count[0] = 0
            dve.wait_ge(s_pack, NB)
            dve.engine_nop().then_inc(s_gap, 1)

            def lt(ins):
                link(ins, s_vt)

            dve.wait_ge(s_cnt, 1)
            lt(dve.tensor_copy(cnt[:, :], COUNT))
            lt(dve.tensor_scalar(cnt_i[:, :], cnt[:, :], float(T - 1), None, ALU.add))
            lt(dve.tensor_scalar(cnt_i[:, :], cnt_i[:, :], T.bit_length() - 1, None, ALU.arith_shift_right))
            lt(dve.tensor_copy(tiles[:, :], cnt_i[:, :]))
            lt(dve.tensor_copy(cum[:, 0, :], tiles[:, :]))
            for n, d in enumerate((1, 2, 4)):
                dve.tensor_copy(cum[:, n + 1, 0:d], cum[:, n, 0:d])
                lt(dve.tensor_tensor(cum[:, n + 1, d:E], cum[:, n, d:E], cum[:, n, 0:E - d], ALU.add))
            lt(dve.tensor_tensor(done[:, :, :], cum[:, 3, :].rearrange("p (o e) -> p o e", o=1).broadcast_to([P, NT, E]),
                                 tau[:, :].rearrange("p (n o) -> p n o", o=1).broadcast_to([P, NT, E]), ALU.is_le))
            lt(dve.tensor_reduce(tab_e[:, :], done[:, :, :], AX, ALU.add))
            lt(dve.tensor_tensor(donec[:, :, :], done[:, :, :],
                                 tiles[:, :].rearrange("p (o e) -> p o e", o=1).broadcast_to([P, NT, E]), ALU.mult))
            lt(dve.tensor_reduce(tab_k[:, :], donec[:, :, :], AX, ALU.add))
            lt(dve.tensor_tensor(tab_k[:, :], tau[:, :], tab_k[:, :], ALU.subtract))
            lt(dve.tensor_scalar(tab_k[:, :], tab_k[:, :], float(T), None, ALU.mult))
            lt(dve.scalar_tensor_tensor(tab_row[:, :], tab_e[:, :], float(RS), tab_k[:, :], ALU.mult, ALU.add))
            dve.tensor_copy(row_of[:, :], tab_row[:, :])
            dve.tensor_scalar(expert_of[:, :], tab_e[:, :], float(E - 1), None, ALU.min)
            dve.tensor_scalar(tab_f[:, :], tab_e[:, :], -1.0, float(E), ALU.mult, ALU.add)
            dve.tensor_tensor(fill_row[:, :], cnt[:, :], region[:, 0, :], ALU.add).then_inc(s_tab, 1)
            dve.wait_ge(s_egap, 1)
            lt(dve.tensor_scalar(wts[:, 1, :], gap[:, :], 1.0, None, ALU.add))
            lt(dve.reciprocal(wts[:, 0, :], wts[:, 1, :]))
            lt(dve.tensor_tensor(wts[:, 1, :], gap[:, :], wts[:, 0, :], ALU.mult))
            dve.wait_ge(s_tab, 1)

            def tile_ids(s, k, load_wait, link_at):
                dve.wait_ge(s_load[k], load_wait)
                ids = back[:, bass.ds(s, 1), :].rearrange("p o h -> p (o h)")
                dve.tensor_scalar(ids, XL[:, k, :, D + 1], tab_f[:, bass.ds(s, 1)], float(TOK), ALU.is_equal,
                                  ALU.mult).then_inc(s_ve, 1)
                dve.wait_ge(s_ve, link_at)
                dve.tensor_tensor(ids, ids, XL[:, k, :, D], ALU.add).then_inc(s_back, 1)

            def split(s, k, made=3):
                for half in range(2):
                    at = slice(half * 2 * T, (half + 1) * 2 * T)
                    dve.wait_ge(s_g, s * 2 + (half + 1))
                    dve.tensor_scalar(hh[:, k, at], hid[:, k, at], scale[:, 2:3], None, ALU.mult).then_inc(s_ve, 1)
                    dve.wait_ge(s_ve, s * 3 + (made + half))
                    dve.scalar_tensor_tensor(hl[:, k, at], hid[:, k, at], scale[:, 2:3], hh[:, k, at],
                                             ALU.mult, ALU.subtract).then_inc(s_split, 1)

            def outputs(u, k, scat_wait):
                e = dve.value_load(expert_of[0:1, bass.ds(u, 1)], min_val=0, max_val=E - 1)
                dve.wait_ge(s_y, u + 1)
                if scat_wait is not None:
                    dve.wait_ge(s_ysc[k], scat_wait)
                bias = b2_rep[:, bass.ds(e * D, D)]
                for half in range(TH):
                    at = slice(half * P, (half + 1) * P)
                    dve.scalar_tensor_tensor(y_sb[:, k, at], Y[k][:, at], inv[:, 1:2], bias, ALU.mult, ALU.add)
                dve.tensor_copy(back_u[:, k, :], back[:, bass.ds(u, 1), :].rearrange("p o h -> p (o h)")
                                ).then_inc(s_ys, 1)

            tile_ids(0, 0, 16, 1)
            for s in range(4):
                if s >= 2:
                    outputs(s - 2, s % 2, None)
                tile_ids(s + 1, (s + 1) % 2, 16 * ((s + 1) // 2 + 1), 3 * s + 2)
                split(s, s % 2)
            with dve.Fori(2, NT // 2 - 1) as r:
                for k in range(2):
                    outputs(r * 2 + (k - 2), k, r * (16 * TH) - 16 * TH)
                    tile_ids(r * 2 + (k + 1), (k + 1) % 2, r * 16 + (16 * k + 16), r * 6 + (3 * k + 2))
                    split(r * 2 + k, k)
            for s in range(NT - 2, NT + 2):
                outputs(s - 2, s % 2, (s // 2 - 1) * 16 * TH)
                if s == NT - 2:
                    tile_ids(s + 1, 1, 16 * (NT // 2), 3 * s + 2)
                if s < NT:
                    split(s, s % 2, 3 if s < NT - 1 else 2)

            def finish(q, k, load_wait, base_):
                dve.wait_ge(s_yl[k], load_wait)
                for c in range(2):
                    for t in range(FT):
                        xt = X[:, bass.ds(q * FT + t, 1), :].rearrange("p o d -> p (o d)")
                        last = dve.scalar_tensor_tensor(xt, yf[:, k, c, t, :], wts[:, c, bass.ds(q * FT + t, 1)], xt,
                                                        ALU.mult, ALU.add)
                    if c == 0:
                        last.then_inc(s_vf, 1)
                        dve.wait_ge(s_vf, base_)
                last.then_inc(s_fin, 1)

            with dve.Fori(0, FC // 2) as r:
                for k in range(2):
                    finish(r * 2 + k, k, r * 32 + 32, r * 2 + (k + 1))


_INS = ["x", "adj", "L0_gnn_W", "L0_gnn_a", "L0_ffn_Wg", "L0_ffn_bg", "L0_ffn_W1", "L0_ffn_b1", "L0_ffn_W2",
        "L0_ffn_b2"]


def kernel(**inputs):
    import numpy as _np
    import concourse.bacc as _bacc
    from concourse import mybir as _mybir
    from concourse.bass_utils import run_bass_kernel_spmd as _run

    nc = _bacc.Bacc("TRN2", target_bir_lowering=False, num_devices=1)
    arrays, args = {}, []
    for name in _INS:
        v = _np.ascontiguousarray(inputs[name])
        arrays[f"in_{name}_dram"] = v
        args.append(nc.dram_tensor(f"in_{name}_dram", v.shape, _mybir.dt.from_np(v.dtype), kind="ExternalInput").ap())
    shape = inputs["x"].shape
    args.append(nc.dram_tensor("out_0_dram", shape, _mybir.dt.float32, kind="ExternalOutput").ap())
    graph_moe(nc, *args)
    r = _run(nc, [arrays], core_ids=[0])
    return r.results[0]["out_0_dram"]
```

```python
from contextlib import ExitStack

import concourse.bass as bass
from concourse import mybir

F32 = mybir.dt.float32
F16 = mybir.dt.float16
BF16 = mybir.dt.bfloat16
I32 = mybir.dt.int32
U32 = mybir.dt.uint32
ALU = mybir.AluOpType
ACT = mybir.ActivationFunctionType
AX = mybir.AxisListType.X
RMAX = bass.bass_isa.ReduceOp.max

P = 128
EPS = 1e-5
SLOPE = 0.2
MASKED = -1e30
REJECT = -3e38
X_SCALE = 1024.0
FAR = 1 << 20


def graph_moe(nc, x, adj, W, a, Wg, bg, W1, b1, W2, b2, out):
    B, N, D = x.shape
    E, _, H = W1.shape
    TOK = B * N
    TT = TOK // P
    GT = N // P
    G = 4
    BT = G * GT
    NB = B // G
    C = H // P
    T = 256
    TH = T // P
    NT = 2 * TOK // T + E
    XS = 8
    NT += -NT % XS
    SPARE = NT - 2 * TOK // T
    RS = TOK + T
    ROW = D + 1
    FC = 8
    FT = TT // FC
    YS = 4
    assert D == P and GT == 2 and C == 4

    x_v = x.rearrange("b (t p) d -> p (b t) d", p=P)
    out_v = out.rearrange("b (t p) d -> p (b t) d", p=P)
    adj_v = adj.rearrange("b (t p) j -> p (b t) j", p=P)
    rows_d = nc.dram_tensor("expert_rows", [E * RS + SPARE * T, ROW], F32).ap()
    y_d = nc.dram_tensor("expert_out", [2 * TOK, D], F32).ap()
    y_v = y_d.rearrange("(k t p) d -> p k t d", k=2, p=P)

    with ExitStack() as ctx:
        def sb(name, shape, dt=F32):
            return ctx.enter_context(nc.sbuf_tensor(name, shape, dt))

        def sem(name):
            return ctx.enter_context(nc.semaphore(name))

        bank = [ctx.enter_context(nc.psum_tensor(f"bank{i}", [P, 512], F32)) for i in range(8)]

        ident = sb("ident", [P, P])
        ident16 = sb("ident16", [P, P], F16)
        ones = sb("ones", [P, P])
        ones16 = sb("ones16", [P, P], BF16)
        before = sb("before", [P, P])
        before16 = sb("before16", [P, P], BF16)
        ramp = sb("ramp", [P, BT, E])
        region = sb("region", [P, BT, E])
        y_row = sb("y_row", [P, 2, TT], U32)
        tau = sb("tau", [P, NT])
        filler = sb("filler", [P, SPARE * TH, ROW])
        w_in = sb("w_in", [P, D])
        wT = sb("wT", [P, D])
        wa = sb("wa", [P, 2])
        wr_rep = sb("wr_rep", [P, P])
        wg = sb("wg", [P, E])
        bg_rep = sb("bg_rep", [P, E])
        b1_in = sb("b1_in", [E * C + 2, P])
        b1T = sb("b1T", [P, E * C + 2])
        b2_rep = sb("b2_rep", [P, E * D])
        wf = sb("wf", [P, 2 * E * H])
        w1f, w2f = wf[:, 0:E * H], wf[:, E * H:2 * E * H]
        w1h = sb("w1h", [P, E * H], F16)
        w1l = sb("w1l", [P, E * H], F16)
        w2h = sb("w2h", [P, E * H], F16)
        w2l = sb("w2l", [P, E * H], F16)
        wmax = sb("wmax", [P, 4])
        wmax_all = sb("wmax_all", [P, 4])
        pow2 = sb("pow2", [P, 4], I32)
        scale = sb("scale", [P, 4])
        inv = sb("inv", [P, 4])
        X = sb("X", [P, TT, D])
        adj_sb = sb("adj_sb", [P, BT, N], I32)
        S = sb("S", [P, BT, N])
        xn = sb("xn", [P, BT, D])
        xn2 = sb("xn2", [P, BT, D])
        stats = sb("stats", [P, 2, BT, 6])
        mv = sb("mv", [P, 2, BT, 2])
        rstd = sb("rstd", [P, 2, BT])
        newton = sb("newton", [P, 2, BT])
        shift = sb("shift", [P, BT])
        xnT = sb("xnT", [P, G, N])
        h_sb = sb("h_sb", [P, G, N])
        pT = sb("pT", [P, G, 2 * N])
        left = sb("left", [P, BT])
        rmax = sb("rmax", [P, BT])
        nsum = sb("nsum", [P, BT])
        negm = sb("negm", [P, BT])
        psum_p = sb("psum_p", [P, BT])
        rsum = sb("rsum", [P, BT])
        pack = sb("pack", [P, 2, BT, ROW])
        lg = sb("lg", [P, BT, E])
        tmp = sb("tmp", [P, BT, E])
        oh1 = sb("oh1", [P, BT, E])
        oh2 = sb("oh2", [P, BT, E])
        picks = sb("picks", [P, BT, E], BF16)
        picks_before = sb("picks_before", [P, E])
        picks_sum = sb("picks_sum", [P, E])
        picks_before16 = sb("picks_before16", [P, E], BF16)
        m1 = sb("m1", [P, BT])
        m2 = sb("m2", [P, BT])
        f1 = sb("f1", [P, BT])
        f2 = sb("f2", [P, BT])
        slot = sb("slot", [P, BT, E])
        target_f = sb("target_f", [P, 2, BT])
        target = sb("target", [P, 2, BT], U32)
        gap = sb("gap", [P, TT])
        wts = sb("wts", [P, 2, TT])
        cnt = sb("cnt", [P, E])
        cnt_i = sb("cnt_i", [P, E], I32)
        tiles = sb("tiles", [P, E])
        cum = sb("cum", [P, 4, E])
        done = sb("done", [P, NT, E])
        donec = sb("donec", [P, NT, E])
        tab_e = sb("tab_e", [P, NT])
        tab_k = sb("tab_k", [P, NT])
        tab_row = sb("tab_row", [P, NT])
        expert_of = sb("expert_of", [P, NT], I32)
        row_of = sb("row_of", [P, NT], I32)
        fill_row = sb("fill_row", [P, E], I32)
        XL = sb("XL", [P, XS, TH, ROW])
        xT = sb("xT", [P, 2, 2 * T], F16)
        hid = sb("hid", [P, 2, C * T])
        hh = sb("hh", [P, 2, C * T], F16)
        hl = sb("hl", [P, 2, C * T], F16)
        y_sb = sb("y_sb", [P, 4, T])
        yf = wf[:, :].rearrange("p (s c t d) -> p s c t d", s=YS, c=2, t=FT)

        s_const = sem("s_const")
        s_wl = sem("s_wl")
        s_ew = sem("s_ew")
        s_filled = sem("s_filled")
        s_x = sem("s_x")
        s_adj = sem("s_adj")
        s_prep_ps = sem("s_prep_ps")
        s_prep = sem("s_prep")
        s_amax = sem("s_amax")
        s_gmax = sem("s_gmax")
        s_scale = sem("s_scale")
        s_whi = sem("s_whi")
        s_wsc = sem("s_wsc")
        s_wlo = sem("s_wlo")
        s_rstd = sem("s_rstd")
        s_xn = sem("s_xn")
        s_t1 = sem("s_t1")
        s_ts1 = sem("s_ts1")
        s_hr = sem("s_hr")
        s_h = sem("s_h")
        s_mask = sem("s_mask")
        s_s = sem("s_s")
        s_negm = sem("s_negm")
        s_sum = sem("s_sum")
        s_leaky = sem("s_leaky")
        s_p = sem("s_p")
        s_pt = sem("s_pt")
        s_pts = sem("s_pts")
        s_av = sem("s_av")
        s_x1 = sem("s_x1")
        s_xn2 = sem("s_xn2")
        s_t2 = sem("s_t2")
        s_ts2 = sem("s_ts2")
        s_lg = sem("s_lg")
        s_picks = sem("s_picks")
        s_rank = sem("s_rank")
        s_misc = sem("s_misc")
        s_pack = sem("s_pack")
        s_pack2 = sem("s_pack2")
        s_turn = sem("s_turn")
        s_scat = sem("s_scat")
        s_packfree = sem("s_packfree")
        s_egap = sem("s_egap")
        s_cnt = sem("s_cnt")
        s_tab = sem("s_tab")
        s_load = [sem(f"s_load{i}") for i in range(XS)]
        s_tt = sem("s_tt")
        s_tts = sem("s_tts")
        s_z = sem("s_z")
        s_g = sem("s_g")
        s_hi = sem("s_hi")
        s_split = sem("s_split")
        s_y = sem("s_y")
        s_ys = sem("s_ys")
        s_ysc = [sem(f"s_ysc{i}") for i in range(4)]
        s_yl = [sem(f"s_yl{i}") for i in range(YS)]
        s_fin0 = sem("s_fin0")
        s_fin = sem("s_fin")
        s_out = sem("s_out")
        s_vturn = sem("s_vturn")
        s_aturn = sem("s_aturn")
        s_sturn = sem("s_sturn")
        s_v = sem("s_v")
        s_vn = sem("s_vn")
        s_va = sem("s_va")
        s_vr = sem("s_vr")
        s_vt = sem("s_vt")

        T_BANK = bank[0]
        HR = [bank[1], bank[2]]
        PT = [bank[3], bank[4]]
        AV = [bank[5], bank[6]]
        MISC = bank[7]
        LEFT = MISC[:, 0:BT]
        LOGITS = MISC[:, 64:64 + BT * E]
        RANK = MISC[:, 128:128 + BT * E]
        COUNT = MISC[:, 192:192 + E]
        TB = [bank[0], bank[7]]
        Z = [[bank[1], bank[2]], [bank[3], bank[4]]]
        Y = [bank[5], bank[6]]

        def experts(eng, s, n):
            return nc.values_load_multi_w_load_instructions(
                expert_of[0:1, bass.ds(s, n)], [eng.engine], min_val=0, max_val=E - 1,
                skip_runtime_bounds_check_because="the tile table is cut off at E - 1")[1]

        block = ctx.enter_context(nc.Block())

        @block.sync
        def _(sp):
            def load_x(b):
                sp.dma_start(X[:, bass.ds(b * BT, BT), :], x_v[:, bass.ds(b * BT, BT), :]).then_inc(s_x, 16)

            def load_adj(b):
                sp.dma_start(adj_sb[:, :, :], adj_v[:, bass.ds(b * BT, BT), :]).then_inc(s_adj, 16)

            for dst, src in ((w_in[:, :], W), (wg[:, :], Wg),
                             (b1_in[0:E * C, :], b1.rearrange("e (c p) -> (e c) p", p=P))):
                sp.dma_start(dst, src).then_inc(s_wl, 16)
            load_x(0)
            load_adj(0)
            sp.wait_ge(s_x, 16)
            load_x(1)
            sp.dma_start(w1f[:, :].rearrange("p (e h) -> p e h", e=E), W1.rearrange("e d h -> d e h")
                         ).then_inc(s_ew, 16)
            sp.dma_start(w2f[:, :].rearrange("p (k d) -> p k d", d=D), W2.rearrange("e (c p) d -> p (e c) d", p=P)
                         ).then_inc(s_ew, 16)
            with sp.Fori(1, NB - 1) as b:
                sp.wait_ge(s_x, b * 16 + 16)
                load_x(b + 1)
                sp.wait_ge(s_mask, b * G)
                load_adj(b)
            sp.wait_ge(s_mask, (NB - 1) * G)
            load_adj(NB - 1)
            sp.wait_ge(s_tab, 1)
            for e in range(E):
                row = sp.value_load(fill_row[0:1, e:e + 1], min_val=0, max_val=E * RS)
                sp.dma_start(rows_d[bass.ds(row, T), :].rearrange("(h p) r -> p h r", p=P),
                             filler[:, 0:TH, :]).then_inc(s_filled, 16)
            sp.wait_ge(s_filled, 16 * (E + 1))
            sp.wait_ge(s_scat, 16 * 2 * BT * NB)

            def load(s, k, wait):
                if wait is not None:
                    sp.wait_ge(s_ysc[k % 4], wait)
                    sp.sem_inc(s_sturn, 1)
                row = sp.value_load(row_of[0:1, bass.ds(s, 1)], min_val=0, max_val=E * RS + SPARE * T - T)
                sp.dma_start(XL[:, k, :, :], rows_d[bass.ds(row, T), :].rearrange("(h p) r -> p h r", p=P)
                             ).then_inc(s_load[k], 16)

            for k in range(XS):
                load(k, k, None)
            with sp.Fori(1, NT // XS) as r:
                for k in range(XS):
                    load(r * XS + k, k, r * (XS // 4 * 16 * TH) + (k // 4 + 1 - XS // 4) * 16 * TH)
            for k in range(4):
                sp.wait_ge(s_ysc[k], 16 * TH * NT // 4)

            def load_y(q, k):
                for c in range(2):
                    sp.dma_start(yf[:, k, c, :, :], y_v[:, c, bass.ds(q * FT, FT), :]).then_inc(s_yl[k], 16)

            for k in range(YS):
                load_y(k, k)
            with sp.Fori(1, FC // YS) as r:
                for k in range(YS):
                    sp.wait_ge(s_fin, r * YS + (k + 1 - YS))
                    load_y(r * YS + k, k)

        @block.gpsimd
        def _(pool):
            pool.memset(ident[:, :], 0.0)
            pool.memset(ones[:, :], 1.0)
            pool.memset(picks_before[:, :], 0.0)
            pool.memset(filler[:, :, 0:D], 0.0)
            pool.iota(filler[:, :, D:D + 1].bitcast(U32), pattern=[[0, SPARE * TH], [0, 1]], base=FAR,
                      channel_multiplier=0).then_inc(s_const, 1)
            pool.wait_ge(s_const, 1)
            pool.affine_select(out=ident[:, :], in_=ident[:, :], compare_op=ALU.not_equal, fill=1.0, base=0,
                               pattern=[[-1, P]], channel_multiplier=1)
            pool.affine_select(out=before[:, :], in_=ones[:, :], compare_op=ALU.is_gt, fill=0.0, base=0,
                               pattern=[[1, P]], channel_multiplier=-1)
            pool.iota(ramp[:, :, :], pattern=[[0, BT], [-1, E]], base=E, channel_multiplier=0,
                      allow_small_or_imprecise_dtypes=True)
            pool.iota(region[:, :, :], pattern=[[0, BT], [RS, E]], base=0, channel_multiplier=0,
                      allow_small_or_imprecise_dtypes=True)
            pool.iota(y_row[:, :, :], pattern=[[TOK, 2], [P, TT]], base=0, channel_multiplier=1)
            pool.iota(tau[:, :], pattern=[[1, NT]], base=0, channel_multiplier=0,
                      allow_small_or_imprecise_dtypes=True).then_inc(s_const, 1)
            pool.wait_ge(s_amax, 1)
            pool.partition_all_reduce(wmax_all[:, :], wmax[:, :], P, RMAX).then_inc(s_gmax, 1)
            for n, (full, hi, lo) in enumerate(((w1f, w1h, w1l), (w2f, w2h, w2l))):
                pool.wait_ge(s_wsc, n + 1)
                pool.tensor_tensor(lo[:, :], full[:, :], hi[:, :], ALU.subtract).then_inc(s_wlo, 1)
            with pool.Fori(0, NB) as b:
                for c, ready in enumerate((s_pack, s_pack2)):
                    pool.wait_ge(ready, b + 1)
                    pool.sem_inc(s_turn, 1)
                    for t in range(BT):
                        pool.indirect_dma_start(
                            rows_d[:, :], bass.IndirectOffsetOnAxis(ap=target[:, c, t:t + 1], axis=0),
                            pack[:, c, t, :], None).then_inc(s_scat, 16)
                pool.wait_ge(s_scat, b * (16 * 2 * BT) + 16 * 2 * BT)
                pool.sem_inc(s_packfree, 1)
            with pool.Fori(0, NT // XS) as r:
                for k in range(XS):
                    pool.wait_ge(s_ys, r * XS + (k + 1))
                    pool.sem_inc(s_turn, 1)
                    for half in range(TH):
                        pool.indirect_dma_start(
                            y_d[:, :],
                            bass.IndirectOffsetOnAxis(ap=XL[:, k, half, D:D + 1].bitcast(U32), axis=0),
                            y_sb[:, k % 4, half * P:(half + 1) * P], None,
                            bounds_check=2 * TOK - 1, oob_is_err=False).then_inc(s_ysc[k % 4], 16)

        @block.scalar
        def _(act):
            act.dma_start(b1_in[E * C:, :], a.rearrange("o (s p) -> (o s) p", p=P)).then_inc(s_wl, 16)
            act.dma_start(bg_rep[:, :], bg.rearrange("(o e) -> o e", o=1).broadcast_to([P, E])).then_inc(s_wl, 16)
            act.dma_start(b2_rep[:, :], b2.rearrange("(o e) d -> o (e d)", o=1).broadcast_to([P, E * D])
                          ).then_inc(s_wl, 16)
            act.wait_ge(s_const, 2)
            act.dma_start(rows_d[E * RS:E * RS + SPARE * T, :].rearrange("(h p) r -> p h r", p=P),
                          filler[:, :, :]).then_inc(s_filled, 16)

            def normalise(b):
                act.wait_ge(s_rstd, b + 1)
                act.sem_inc(s_aturn, 1)
                for t in range(BT):
                    last = act.activation(xn[:, t, :], X[:, bass.ds(b * BT + t, 1), :], ACT.Identity,
                                          bias=shift[:, t:t + 1], scale=rstd[:, 0, t:t + 1])
                    if t % GT == GT - 1:
                        last.then_inc(s_xn, 1)

            def turned_first(i, g):
                act.wait_ge(s_t1, i * G + (g + 1))
                act.activation(xnT[:, g, :], T_BANK[:, 0:N], ACT.Copy).then_inc(s_ts1, 1)

            def turned_probs(j, g):
                act.wait_ge(s_pt, j * G + (g + 1))
                act.activation(pT[:, g, :], PT[g % 2][:, :], ACT.Copy).then_inc(s_pts, 1)

            def copy_h(i, g):
                act.wait_ge(s_hr, i * G + (g + 1))
                act.activation(h_sb[:, g, :], HR[g % 2][:, 0:N], ACT.Copy).then_inc(s_h, 1)

            def add_left(i):
                act.wait_ge(s_negm, i + 1)
                for g in range(G):
                    for t in range(g * GT, (g + 1) * GT):
                        last = act.activation(S[:, t, :], S[:, t, :], ACT.Identity, bias=left[:, t:t + 1])
                    last.then_inc(s_sum, 1)

            def probs(i, g):
                act.wait_ge(s_leaky, i * G + (g + 1))
                for t in range(g * GT, (g + 1) * GT):
                    last = act.activation(S[:, t, :], S[:, t, :], ACT.Exp, bias=negm[:, t:t + 1],
                                          accum_out=psum_p[:, t:t + 1])
                last.then_inc(s_p, 1)

            def turned_second(j, g):
                act.wait_ge(s_t2, j * G + (g + 1))
                act.activation(xnT[:, g, :], T_BANK[:, 0:N], ACT.Copy).then_inc(s_ts2, 1)

            def second_pack(j):
                act.wait_ge(s_pack, j + 1)
                act.activation(pack[:, 1, :, 0:D], pack[:, 0, :, 0:D], ACT.Copy).then_inc(s_pack2, 1)

            def batch(i, j, more):
                for g in range(G + 1):
                    if j is not None and g < G:
                        turned_probs(j, g)
                    if i is not None and g < G:
                        turned_first(i, g)
                    if i is not None and g >= 1:
                        copy_h(i, g - 1)
                if i is not None:
                    add_left(i)
                if more:
                    normalise(i + 1)
                for g in range(G):
                    if j is not None:
                        turned_second(j, g)
                    if i is not None:
                        probs(i, g)
                if j is not None:
                    second_pack(j)

            normalise(0)
            batch(0, None, True)
            act.wait_ge(s_scale, 1)
            for n, (full, hi) in enumerate(((w1f, w1h), (w2f, w2h))):
                act.activation(hi[:, :], full[:, :], ACT.Copy, scale=scale[:, n:n + 1]).then_inc(s_whi, 1)
                act.wait_ge(s_whi, n + 1)
                act.activation(full[:, :], full[:, :], ACT.Copy, scale=scale[:, n:n + 1]).then_inc(s_wsc, 1)
            with act.Fori(1, NB - 1) as i:
                batch(i, i - 1, True)
            batch(NB - 1, NB - 2, False)
            batch(None, NB - 1, False)
            act.activation(gap[:, :], gap[:, :], ACT.Exp).then_inc(s_egap, 1)

            act.wait_ge(s_tab, 1)

            def turned_tile(s, k):
                act.wait_ge(s_tt, s + 1)
                act.activation(xT[:, k % 2, :], TB[k % 2][:, 0:T].bitcast(F16), ACT.Copy).then_inc(s_tts, 1)

            def gelu(s, k, e, wait):
                k %= 2
                for c in range(C):
                    if c % 2 == 0:
                        act.wait_ge(s_z, s * 2 + (c // 2 + 1))
                        if wait:
                            act.wait_ge(s_split, s * 2 + (c // 2 - 3))
                        act.sem_inc(s_aturn, 1)
                    ins = act.activation(hid[:, k, c * T:(c + 1) * T], Z[k][c // 2][:, (c % 2) * T:(c % 2 + 1) * T],
                                         ACT.Gelu, bias=b1T[:, bass.ds(e * C + c, 1)], scale=inv[:, 0:1])
                    if c % 2 == 1:
                        ins.then_inc(s_g, 1)

            def tiles_of(s0, wait, last):
                es = experts(act, s0, 4)
                for k in range(4):
                    if not (last and k == 3):
                        turned_tile(s0 + (k + 1), k + 1)
                    gelu(s0 + k, k, es[k], wait or k >= 2)

            turned_tile(0, 0)
            tiles_of(0, False, False)
            with act.Fori(1, NT // 4 - 1) as r:
                tiles_of(r * 4, True, False)
            tiles_of(NT - 4, True, True)

            with act.Fori(0, FC) as q:
                act.wait_ge(s_fin, q + 1)
                act.dma_start(out_v[:, bass.ds(q * FT, FT), :], X[:, bass.ds(q * FT, FT), :]).then_inc(s_out, 16)
            act.wait_ge(s_out, 16 * FC)

        @block.tensor
        def _(pe):
            pe.wait_ge(s_const, 2)
            pe.wait_ge(s_wl, 16 * 6)
            pe.transpose(T_BANK[:, 0:D], w_in[:, :], ident[:, :])
            pe.transpose(T_BANK[:, 256:256 + E * C + 2], b1_in[:, :], ident[0:E * C + 2, 0:E * C + 2]
                         ).then_inc(s_prep_ps, 1)
            pe.wait_ge(s_prep, 1)
            pe.matmul(T_BANK[:, 128:130], w_in[:, :], b1T[:, E * C:], start=True, stop=True).then_inc(s_prep_ps, 1)
            pe.wait_ge(s_prep, 2)


            def turn_first(i, g):
                pe.wait_ge(s_xn, i * G + (g + 1))
                if g:
                    pe.wait_ge(s_ts1, i * G + g)
                for t in range(GT):
                    last = pe.transpose(T_BANK[:, t * P:(t + 1) * P], xn[:, g * GT + t, :], ident[:, :])
                last.then_inc(s_t1, 1)

            def project(i, g, first):
                hr = HR[g % 2]
                pe.wait_ge(s_ts1, i * G + (g + 1))
                if g >= 2:
                    pe.wait_ge(s_s, i * G + (g - 1))
                for t in range(GT):
                    pe.matmul(hr[:, t * P:(t + 1) * P], xnT[:, g, t * P:(t + 1) * P], wT[:, :], start=True, stop=True)
                if g == 0 and not first:
                    pe.wait_ge(s_misc, i)
                for t in range(GT):
                    pe.matmul(LEFT[:, g * GT + t:g * GT + t + 1], xnT[:, g, t * P:(t + 1) * P], wa[:, 0:1],
                              start=True, stop=True)
                pe.matmul(hr[:, N:2 * N], wr_rep[:, :], xnT[:, g, :], start=True, stop=True).then_inc(s_hr, 1)

            def turn_probs(j, g):
                pe.wait_ge(s_p, j * G + (g + 1))
                if g >= 2:
                    pe.wait_ge(s_pts, j * G + (g - 1))
                for n in range(GT):
                    for t in range(GT):
                        last = pe.transpose(PT[g % 2][:, n * N + t * P:n * N + (t + 1) * P],
                                            S[:, g * GT + t, n * P:(n + 1) * P], ident[:, :])
                last.then_inc(s_pt, 1)

            def attend(j, g):
                pe.wait_ge(s_pts, j * G + (g + 1))
                if g >= 2:
                    pe.wait_ge(s_x1, j * G + (g - 1))
                for t in range(GT):
                    for n in range(GT):
                        last = pe.matmul(AV[g % 2][:, t * P:(t + 1) * P],
                                         pT[:, g, n * N + t * P:n * N + (t + 1) * P],
                                         h_sb[:, g, n * P:(n + 1) * P], start=(n == 0), stop=(n == GT - 1))
                last.then_inc(s_av, 1)

            def turn_second(j, g):
                pe.wait_ge(s_xn2, j * G + (g + 1))
                if g:
                    pe.wait_ge(s_ts2, j * G + g)
                for t in range(GT):
                    last = pe.transpose(T_BANK[:, t * P:(t + 1) * P], xn2[:, g * GT + t, :], ident[:, :])
                last.then_inc(s_t2, 1)

            def route(j, g):
                pe.wait_ge(s_ts2, j * G + (g + 1))
                for t in range(GT):
                    n = (g * GT + t) * E
                    last = pe.matmul(LOGITS[:, n:n + E], xnT[:, g, t * P:(t + 1) * P], wg[:, :], start=True, stop=True)
                if g == G - 1:
                    last.then_inc(s_lg, 1)

            def rank(j):
                pe.wait_ge(s_picks, j + 1)
                flat = picks[:, :, :].rearrange("p t e -> p (t e)")
                pe.matmul(RANK[:, :], before16[:, :], flat, start=True, stop=False)
                for t in range(1, BT):
                    pe.matmul(RANK[:, t * E:], ones16[:, :], flat[:, 0:(BT - t) * E], start=False, stop=False)
                pe.matmul(RANK[:, :].rearrange("p (t e) -> p t e", e=E), ones16[:, :],
                          picks_before16[:, :].rearrange("p (o e) -> p o e", o=1).broadcast_to([P, BT, E]),
                          start=False, stop=True).then_inc(s_rank, 1)

            def batch(i, j):
                for g in range(G + 1):
                    if j is not None and g < G:
                        turn_probs(j, g)
                    if i is not None and g < G:
                        turn_first(i, g)
                    if j is not None and g >= 1:
                        attend(j, g - 1)
                    if i is not None and g >= 1:
                        project(i, g - 1, j is None)
                if j is not None:
                    if i is not None:
                        pe.wait_ge(s_negm, i + 1)
                    for g in range(G + 1):
                        if g < G:
                            turn_second(j, g)
                        if g >= 1:
                            route(j, g - 1)
                    rank(j)

            batch(0, None)
            with pe.Fori(1, NB) as i:
                batch(i, i - 1)
            batch(None, NB - 1)
            pe.wait_ge(s_pack, NB)
            pe.matmul(COUNT, ones16[:, :], picks_before16[:, :], start=True, stop=True).then_inc(s_cnt, 1)

            pe.wait_ge(s_tab, 1)
            pe.wait_ge(s_wlo, 2)

            def turn_tile(s, k, landed):
                pe.wait_ge(s_load[k], landed)
                parts = XL[:, k, :, :].bitcast(F16)
                tb = TB[k % 2][:, 0:T].bitcast(F16)
                for part in range(2):
                    for half in range(TH):
                        last = pe.transpose(tb[:, part * T + half * P:part * T + (half + 1) * P],
                                            parts[:, half, part * D:(part + 1) * D], ident16[:, :])
                last.then_inc(s_tt, 1)

            def hidden(s, k, e, wait):
                k %= 2
                pe.wait_ge(s_tts, s + 1)
                for c in range(C):
                    if wait and c % 2 == 0:
                        pe.wait_ge(s_g, s * 2 + (c // 2 - 3))
                    z = Z[k][c // 2][:, (c % 2) * T:(c % 2 + 1) * T]
                    hi = w1h[:, bass.ds(e * H + c * P, P)]
                    lo = w1l[:, bass.ds(e * H + c * P, P)]
                    pe.matmul(z, hi, xT[:, k, 0:T], start=True, stop=False)
                    pe.matmul(z, hi, xT[:, k, T:2 * T], start=False, stop=False)
                    last = pe.matmul(z, lo, xT[:, k, 0:T], start=False, stop=True)
                    if c % 2 == 1:
                        last.then_inc(s_z, 1)

            def output(u, k, e, wait):
                k %= 2
                pe.wait_ge(s_split, u * 2 + 2)
                if wait:
                    pe.wait_ge(s_ys, u - 1)
                for half in range(TH):
                    y = Y[k][:, half * P:(half + 1) * P]
                    for c in range(C):
                        at = slice(c * T + half * P, c * T + (half + 1) * P)
                        hi = w2h[:, bass.ds(e * H + c * P, P)]
                        lo = w2l[:, bass.ds(e * H + c * P, P)]
                        pe.matmul(y, hh[:, k, at], hi, start=(c == 0), stop=False)
                        pe.matmul(y, hh[:, k, at], lo, start=False, stop=False)
                        last = pe.matmul(y, hl[:, k, at], hi, start=False, stop=(c == C - 1))
                last.then_inc(s_y, 1)

            turn_tile(0, 0, 16)
            es = experts(pe, 0, XS)
            for s in range(XS):
                if s >= 2:
                    output(s - 2, s - 2, es[s - 2], s >= 4)
                turn_tile(s + 1, (s + 1) % XS, 16 * ((s + 1) // XS + 1))
                hidden(s, s, es[s], s >= 2)

            def tiles_of(r, s0, last):
                for k in range(XS):
                    if k % 4 == 0:
                        es = experts(pe, s0 + k - 2, 6)
                    output(s0 + (k - 2), k, es[k % 4], True)
                    if not (last and k == XS - 1):
                        turn_tile(s0 + (k + 1), (k + 1) % XS, r * 16 + 16 * ((k + 1) // XS + 1))
                    hidden(s0 + k, k, es[k % 4 + 2], True)

            with pe.Fori(1, NT // XS - 1) as r:
                tiles_of(r, r * XS, False)
            tiles_of(NT // XS - 1, NT - XS, True)
            es = experts(pe, NT - 2, 2)
            for k in range(2):
                output(NT - 2 + k, k, es[k], True)

        @block.vector
        def _(dve):
            count = [0]

            def link(ins, sem_, base=0):
                count[0] += 1
                ins.then_inc(sem_, 1)
                dve.wait_ge(sem_, base + count[0])

            dve.sem_inc(s_packfree, 1)
            dve.sem_inc(s_misc, 1)
            dve.wait_ge(s_const, 2)
            dve.tensor_copy(ident16[:, :], ident[:, :])
            dve.tensor_copy(ones16[:, :], ones[:, :])
            dve.tensor_copy(before16[:, :], before[:, :])
            dve.memset(picks_before16[:, :], 0.0)
            dve.wait_ge(s_prep_ps, 1)
            dve.tensor_copy(wT[:, :], T_BANK[:, 0:D])
            dve.tensor_copy(b1T[:, :], T_BANK[:, 256:256 + E * C + 2]).then_inc(s_prep, 1)
            dve.wait_ge(s_prep_ps, 2)
            link(dve.tensor_copy(wa[:, :], T_BANK[:, 128:130]), s_v)
            dve.tensor_scalar(wr_rep[:, :], ones[:, :], wa[:, 1:2], None, ALU.mult).then_inc(s_prep, 1)

            class Own:
                def __init__(self, sem_, each):
                    self.sem, self.each = sem_, each

                def begin(self, start):
                    self.start, self.n = start, 0

                def __call__(self, ins):
                    self.n += 1
                    ins.then_inc(self.sem, 1)
                    dve.wait_ge(self.sem, self.start + self.n)

                def end(self):
                    assert self.n == self.each, self.n

            NORM, ATT, ROUT = 15, 2, 21
            norm, att, rout = Own(s_vn, NORM), Own(s_va, ATT), Own(s_vr, ROUT)

            def statistics(which, b):
                for t in range(BT):
                    last = dve.bn_stats(stats[:, which, t, :], X[:, bass.ds(b * BT + t, 1), :])
                return last

            def factors(which, last):
                norm(last)
                dve.sem_inc(s_vturn, 1)
                for w in which:
                    for t in range(BT):
                        last = dve.bn_aggr(mv[:, w, t, :], stats[:, w, t, :])
                norm(last)
                at = slice(which[0], which[-1] + 1)
                var, r, n = mv[:, at, :, 1], rstd[:, at, :], newton[:, at, :]
                norm(dve.tensor_scalar(var, var, EPS, float(1 << 26), ALU.add, ALU.mult))
                norm(dve.tensor_scalar(r.bitcast(I32), var.bitcast(I32), 1, None, ALU.logical_shift_right))
                norm(dve.tensor_scalar(r.bitcast(I32), r.bitcast(I32), -1.0, float(0x5F3759DF), ALU.mult, ALU.add))
                for grown in (1.0, 2.0, 16.0):
                    norm(dve.tensor_tensor(n, r, var, ALU.mult))
                    norm(dve.tensor_tensor(n, n, r, ALU.mult))
                    norm(dve.scalar_tensor_tensor(r, n, 3.0 * grown * grown, r, ALU.subtract, ALU.mult,
                                                  reverse0=True))
                if 0 in which:
                    norm(dve.scalar_tensor_tensor(shift[:, :], mv[:, 0, :, 0], -1.0, rstd[:, 0, :],
                                                  ALU.mult, ALU.mult))
                    dve.sem_inc(s_rstd, 1)

            def mask(i, j, g):
                if g == 0:
                    dve.wait_ge(s_adj, i * 16 + 16)
                if j is not None:
                    dve.wait_ge(s_pt, j * G + (g + 1))
                at = slice(g * GT, (g + 1) * GT)
                dve.tensor_scalar(S[:, at, :], adj_sb[:, at, :], 0.0, MASKED, ALU.is_equal, ALU.mult
                                  ).then_inc(s_mask, 1)

            def right_scores(i, g):
                dve.wait_ge(s_mask, i * G + (g + 1))
                dve.wait_ge(s_h, i * G + (g + 1))
                dve.sem_inc(s_vturn, 1)
                for t in range(g * GT, (g + 1) * GT):
                    last = dve.tensor_tensor_reduce(S[:, t, :], S[:, t, :], HR[g % 2][:, N:2 * N], 1.0, -3e38,
                                                    ALU.add, ALU.max, rmax[:, t:t + 1])
                last.then_inc(s_s, 1)

            def row_maxima(i):
                att(dve.tensor_copy(left[:, :], LEFT))
                dve.wait_ge(s_s, i * G + G)
                att(dve.scalar_tensor_tensor(nsum[:, :], rmax[:, :], -1.0, left[:, :], ALU.mult, ALU.subtract))
                dve.scalar_tensor_tensor(negm[:, :], nsum[:, :], SLOPE, nsum[:, :], ALU.mult, ALU.min
                                         ).then_inc(s_negm, 1)

            def leaky(i, g):
                dve.wait_ge(s_sum, i * G + (g + 1))
                both = S[:, g * GT:(g + 1) * GT, :]
                dve.scalar_tensor_tensor(both, both, SLOPE, both, ALU.mult, ALU.max).then_inc(s_leaky, 1)

            def residual(j, g):
                dve.wait_ge(s_av, j * G + (g + 1))
                for t in range(g * GT, (g + 1) * GT):
                    xt = X[:, bass.ds(j * BT + t, 1), :].rearrange("p o d -> p (o d)")
                    last = dve.scalar_tensor_tensor(xt, AV[g % 2][:, (t % GT) * P:(t % GT + 1) * P],
                                                    rsum[:, t:t + 1], xt, ALU.mult, ALU.add)
                last.then_inc(s_x1, 1)

            def second_norm(j):
                for t in range(BT):
                    last = dve.tensor_scalar(xn2[:, t, :], X[:, bass.ds(j * BT + t, 1), :], mv[:, 1, t, 0:1],
                                             rstd[:, 1, t:t + 1], ALU.subtract, ALU.mult)
                    if t % GT == GT - 1:
                        last.then_inc(s_xn2, 1)

            def over_e(v):
                return v[:, :].rearrange("p (t o) -> p t o", o=1).broadcast_to([P, BT, E])

            def choose(oh, m, f):
                rout(dve.tensor_reduce(m[:, :], lg[:, :, :], AX, ALU.max))
                rout(dve.tensor_tensor(tmp[:, :, :], lg[:, :, :], over_e(m), ALU.is_equal))
                rout(dve.tensor_tensor(tmp[:, :, :], tmp[:, :, :], ramp[:, :, :], ALU.mult))
                rout(dve.tensor_reduce(f[:, :], tmp[:, :, :], AX, ALU.max))
                rout(dve.tensor_tensor(oh[:, :, :], ramp[:, :, :], over_e(f), ALU.is_equal))

            def router(j):
                dve.wait_ge(s_lg, j + 1)
                rout(dve.tensor_tensor(lg[:, :, :], LOGITS.rearrange("p (t e) -> p t e", e=E),
                                       bg_rep[:, :].rearrange("p (o e) -> p o e", o=1).broadcast_to([P, BT, E]),
                                       ALU.add))
                choose(oh1, m1, f1)
                rout(dve.scalar_tensor_tensor(lg[:, :, :], oh1[:, :, :], REJECT, lg[:, :, :], ALU.mult, ALU.add))
                choose(oh2, m2, f2)
                dve.tensor_tensor(picks[:, :, :], oh1[:, :, :], oh2[:, :, :], ALU.add).then_inc(s_picks, 1)
                dve.tensor_tensor(gap[:, bass.ds(j * BT, BT)], m2[:, :], m1[:, :], ALU.subtract)
                hi = pack[:, 0, :, 0:D // 2].bitcast(F16)
                lo = pack[:, 0, :, D // 2:D].bitcast(F16)
                dve.wait_ge(s_packfree, j + 1)
                rout(dve.tensor_scalar(hi, xn2[:, :, :], X_SCALE, None, ALU.mult))
                dve.scalar_tensor_tensor(lo, xn2[:, :, :], X_SCALE, hi, ALU.mult, ALU.subtract)
                dve.tensor_copy(pack[:, :, :, D].bitcast(U32), y_row[:, :, bass.ds(j * BT, BT)])
                dve.wait_ge(s_picks, j + 1)
                rout(dve.tensor_reduce(picks_sum[:, :], picks[:, :, :].rearrange("p t e -> p e t"), AX, ALU.add))
                rout(dve.tensor_tensor(picks_before[:, :], picks_before[:, :], picks_sum[:, :], ALU.add))
                dve.wait_ge(s_rank, j + 1)
                dve.tensor_copy(picks_before16[:, :], picks_before[:, :])
                rout(dve.tensor_tensor(slot[:, :, :], RANK.rearrange("p (t e) -> p t e", e=E), region[:, :, :],
                                       ALU.add))
                dve.sem_inc(s_misc, 1)
                rout(dve.tensor_tensor(oh1[:, :, :], oh1[:, :, :], slot[:, :, :], ALU.mult))
                rout(dve.tensor_reduce(target_f[:, 0, :], oh1[:, :, :], AX, ALU.add))
                rout(dve.tensor_tensor(oh2[:, :, :], oh2[:, :, :], slot[:, :, :], ALU.mult))
                rout(dve.tensor_reduce(target_f[:, 1, :], oh2[:, :, :], AX, ALU.add))
                dve.tensor_copy(target[:, :, :], target_f[:, :, :]).then_inc(s_pack, 1)

            def batch(i, j, more):
                if i is not None:
                    att.begin(i * ATT)
                if j is not None:
                    rout.begin(j * ROUT)
                if more:
                    dve.wait_ge(s_x, i * 16 + 32)
                    dve.sem_inc(s_vturn, 1)
                    last = statistics(0, i + 1)
                if j is not None:
                    dve.wait_ge(s_p, j * G + G)
                    rout(dve.reciprocal(rsum[:, :], psum_p[:, :]))
                for g in range(G + 1):
                    if i is not None and g < G:
                        mask(i, j, g)
                    if j is not None and g >= 1:
                        residual(j, g - 1)
                    if i is not None and g >= 1:
                        right_scores(i, g - 1)
                if i is not None:
                    row_maxima(i)
                if j is not None:
                    dve.wait_ge(s_x1, j * G + G)
                    dve.sem_inc(s_vturn, 1)
                    last = statistics(1, j)
                if more:
                    dve.wait_ge(s_xn, i * G + G)
                factors(([0] if more else []) + ([1] if j is not None else []), last)
                if j is not None:
                    second_norm(j)
                if i is not None:
                    for g in range(G):
                        leaky(i, g)
                if j is not None:
                    router(j)

            norm.begin(0)
            dve.wait_ge(s_x, 16)
            factors([0], statistics(0, 0))
            norm.begin(NORM)
            batch(0, None, True)
            dve.wait_ge(s_ew, 32)
            dve.tensor_reduce(wmax[:, 0:1], w1f[:, :], AX, ALU.max, apply_absolute_value=True)
            dve.tensor_reduce(wmax[:, 1:2], w2f[:, :], AX, ALU.max, apply_absolute_value=True)
            link(dve.tensor_reduce(wmax[:, 2:3], b1T[:, 0:E * C], AX, ALU.max, apply_absolute_value=True), s_v)
            dve.tensor_copy(wmax[:, 3:4], wmax[:, 2:3]).then_inc(s_amax, 1)
            dve.wait_ge(s_gmax, 1)
            link(dve.scalar_tensor_tensor(wmax_all[:, 2:3], wmax_all[:, 0:1], float(D), wmax_all[:, 2:3],
                                          ALU.mult, ALU.add), s_v)
            link(dve.tensor_scalar(wmax_all[:, :], wmax_all[:, :], 1e-12, None, ALU.max), s_v)
            link(dve.tensor_scalar(pow2[:, :], wmax_all[:, :].bitcast(I32), 0x7F800000, None, ALU.bitwise_and), s_v)
            link(dve.tensor_scalar(scale[:, :].bitcast(I32), pow2[:, :], -1.0, float((254 + 13) << 23),
                                   ALU.mult, ALU.add), s_v)
            link(dve.tensor_scalar(inv[:, :].bitcast(I32), scale[:, :].bitcast(I32), -1.0, float(254 << 23),
                                   ALU.mult, ALU.add), s_v)
            dve.tensor_tensor(inv[:, 1:2], inv[:, 1:2], inv[:, 2:3], ALU.mult)
            dve.tensor_scalar(inv[:, 0:1], inv[:, 0:1], 1.0 / X_SCALE, None, ALU.mult).then_inc(s_scale, 1)

            with dve.Fori(1, NB - 1) as i:
                norm.begin(i * NORM + NORM)
                batch(i, i - 1, True)
                norm.end(), att.end(), rout.end()
            norm.begin(NB * NORM)
            batch(NB - 1, NB - 2, False)
            norm.begin(NB * NORM + NORM - 1)
            batch(None, NB - 1, False)

            count[0] = 0

            def lt(ins):
                link(ins, s_vt)

            dve.wait_ge(s_cnt, 1)
            lt(dve.tensor_copy(cnt[:, :], COUNT))
            lt(dve.tensor_scalar(cnt_i[:, :], cnt[:, :], float(T - 1), None, ALU.add))
            lt(dve.tensor_scalar(cnt_i[:, :], cnt_i[:, :], T.bit_length() - 1, None, ALU.arith_shift_right))
            lt(dve.tensor_copy(tiles[:, :], cnt_i[:, :]))
            lt(dve.tensor_copy(cum[:, 0, :], tiles[:, :]))
            for n, d in enumerate((1, 2, 4)):
                dve.tensor_copy(cum[:, n + 1, 0:d], cum[:, n, 0:d])
                lt(dve.tensor_tensor(cum[:, n + 1, d:E], cum[:, n, d:E], cum[:, n, 0:E - d], ALU.add))
            lt(dve.tensor_tensor(done[:, :, :], cum[:, 3, :].rearrange("p (o e) -> p o e", o=1).broadcast_to([P, NT, E]),
                                 tau[:, :].rearrange("p (n o) -> p n o", o=1).broadcast_to([P, NT, E]), ALU.is_le))
            lt(dve.tensor_reduce(tab_e[:, :], done[:, :, :], AX, ALU.add))
            lt(dve.tensor_tensor(donec[:, :, :], done[:, :, :],
                                 tiles[:, :].rearrange("p (o e) -> p o e", o=1).broadcast_to([P, NT, E]), ALU.mult))
            lt(dve.tensor_reduce(tab_k[:, :], donec[:, :, :], AX, ALU.add))
            lt(dve.tensor_tensor(tab_k[:, :], tau[:, :], tab_k[:, :], ALU.subtract))
            lt(dve.tensor_scalar(tab_k[:, :], tab_k[:, :], float(T), None, ALU.mult))
            lt(dve.scalar_tensor_tensor(tab_row[:, :], tab_e[:, :], float(RS), tab_k[:, :], ALU.mult, ALU.add))
            dve.tensor_copy(row_of[:, :], tab_row[:, :])
            dve.tensor_scalar(expert_of[:, :], tab_e[:, :], float(E - 1), None, ALU.min)
            dve.tensor_tensor(fill_row[:, :], cnt[:, :], region[:, 0, :], ALU.add).then_inc(s_tab, 1)
            dve.wait_ge(s_egap, 1)
            lt(dve.tensor_scalar(wts[:, 1, :], gap[:, :], 1.0, None, ALU.add))
            lt(dve.reciprocal(wts[:, 0, :], wts[:, 1, :]))
            lt(dve.tensor_tensor(wts[:, 1, :], gap[:, :], wts[:, 0, :], ALU.mult))
            dve.wait_ge(s_tab, 1)

            def split(s, k):
                k %= 2
                for half in range(2):
                    at = slice(half * 2 * T, (half + 1) * 2 * T)
                    dve.wait_ge(s_g, s * 2 + (half + 1))
                    dve.tensor_scalar(hh[:, k, at], hid[:, k, at], scale[:, 2:3], None, ALU.mult).then_inc(s_hi, 1)
                    dve.wait_ge(s_hi, s * 2 + (half + 1))
                    dve.scalar_tensor_tensor(hl[:, k, at], hid[:, k, at], scale[:, 2:3], hh[:, k, at],
                                             ALU.mult, ALU.subtract).then_inc(s_split, 1)

            def outputs(u, k, e, scattered):
                dve.wait_ge(s_y, u + 1)
                if scattered is not None:
                    dve.wait_ge(s_ysc[k], scattered)
                both = [v.rearrange("p (h d) -> p h d", d=D) for v in (y_sb[:, k, :], Y[k % 2][:, 0:T])]
                bias = b2_rep[:, bass.ds(e * D, D)].rearrange("p (o d) -> p o d", o=1).broadcast_to([P, TH, D])
                dve.scalar_tensor_tensor(both[0], both[1], inv[:, 1:2], bias, ALU.mult, ALU.add).then_inc(s_ys, 1)

            es = experts(dve, 0, 2)
            for s in range(4):
                if s >= 2:
                    outputs(s - 2, s - 2, es[s - 2], None)
                split(s, s)

            def tiles_of(s0, before_):
                es = experts(dve, s0 - 2, 4)
                for k in range(4):
                    slot_ = (k + 2) % 4
                    outputs(s0 + (k - 2), slot_, es[k],
                            None if before_ is None else before_[0] if slot_ < 2 else before_[1])
                    split(s0 + k, k)

            es = experts(dve, 2, 4)
            for k in range(4):
                slot_ = (k + 2) % 4
                outputs(2 + k, slot_, es[k], 16 * TH if slot_ < 2 else None)
                split(4 + k, k)
            with dve.Fori(2, NT // 4) as r:
                tiles_of(r * 4, (r * (16 * TH), r * (16 * TH) - 16 * TH))
            es = experts(dve, NT - 2, 2)
            for k in range(2):
                outputs(NT - 2 + k, 2 + k, es[k], (NT // 4 - 1) * 16 * TH)

            def finish(q, k, loaded):
                dve.wait_ge(s_yl[k], loaded)
                for c, done_ in enumerate((s_fin0, s_fin)):
                    if c:
                        dve.wait_ge(s_fin0, q + 1)
                    for t in range(FT):
                        xt = X[:, bass.ds(q * FT + t, 1), :].rearrange("p o d -> p (o d)")
                        last = dve.scalar_tensor_tensor(xt, yf[:, k, c, t, :], wts[:, c, bass.ds(q * FT + t, 1)], xt,
                                                        ALU.mult, ALU.add)
                    last.then_inc(done_, 1)

            with dve.Fori(0, FC // YS) as r:
                for k in range(YS):
                    finish(r * YS + k, k, r * 32 + 32)


_INS = ["x", "adj", "L0_gnn_W", "L0_gnn_a", "L0_ffn_Wg", "L0_ffn_bg", "L0_ffn_W1", "L0_ffn_b1", "L0_ffn_W2",
        "L0_ffn_b2"]


def kernel(**inputs):
    import numpy as _np
    import concourse.bacc as _bacc
    from concourse import mybir as _mybir
    from concourse.bass_utils import run_bass_kernel_spmd as _run

    nc = _bacc.Bacc("TRN2", target_bir_lowering=False, num_devices=1)
    arrays, args = {}, []
    for name in _INS:
        v = _np.ascontiguousarray(inputs[name])
        arrays[f"in_{name}_dram"] = v
        args.append(nc.dram_tensor(f"in_{name}_dram", v.shape, _mybir.dt.from_np(v.dtype), kind="ExternalInput").ap())
    shape = inputs["x"].shape
    args.append(nc.dram_tensor("out_0_dram", shape, _mybir.dt.float32, kind="ExternalOutput").ap())
    graph_moe(nc, *args)
    r = _run(nc, [arrays], core_ids=[0])
    return r.results[0]["out_0_dram"]
```

```python
from contextlib import ExitStack

import concourse.bass as bass
from concourse import mybir

F32 = mybir.dt.float32
F16 = mybir.dt.float16
BF16 = mybir.dt.bfloat16
I32 = mybir.dt.int32
U32 = mybir.dt.uint32
ALU = mybir.AluOpType
ACT = mybir.ActivationFunctionType
AX = mybir.AxisListType.X
RMAX = bass.bass_isa.ReduceOp.max

P = 128
EPS = 1e-5
SLOPE = 0.2
MASKED = -1e30
REJECT = -3e38
X_SCALE = 1024.0
FAR = 1 << 20


def graph_moe(nc, x, adj, W, a, Wg, bg, W1, b1, W2, b2, out):
    B, N, D = x.shape
    E, _, H = W1.shape
    TOK = B * N
    TT = TOK // P
    GT = N // P
    G = 4
    BT = G * GT
    Q = G // 2
    NB = B // G
    C = H // P
    T = 256
    TH = T // P
    NT = (2 * TOK + E * (T - 1)) // T
    XS = 8
    TAB = NT + -NT % XS
    SPARE = NT - 2 * TOK // T
    RS = TOK + T
    ROW = D + 1
    LAG = 3
    FC = 16
    FT = TT // FC
    YS = 8
    assert D == P and GT == 2 and C == 4 and NT % 4 and NT % XS > LAG

    x_v = x.rearrange("b (t p) d -> p (b t) d", p=P)
    out_v = out.rearrange("b (t p) d -> p (b t) d", p=P)
    adj_v = adj.rearrange("b (t p) j -> p (b t) j", p=P)
    rows_d = nc.dram_tensor("expert_rows", [E * RS + SPARE * T, ROW], F32).ap()
    y_d = nc.dram_tensor("expert_out", [2 * TOK, D], F32).ap()
    y_v = y_d.rearrange("(k t p) d -> p k t d", k=2, p=P)

    with ExitStack() as ctx:
        def sb(name, shape, dt=F32):
            return ctx.enter_context(nc.sbuf_tensor(name, shape, dt))

        def sem(name):
            return ctx.enter_context(nc.semaphore(name))

        bank = [ctx.enter_context(nc.psum_tensor(f"bank{i}", [P, 512], F32)) for i in range(8)]

        ident = sb("ident", [P, P])
        ident16 = sb("ident16", [P, P], F16)
        ones = sb("ones", [P, P])
        ones16 = sb("ones16", [P, P], BF16)
        before = sb("before", [P, P])
        before16 = sb("before16", [P, P], BF16)
        ramp = sb("ramp", [P, BT, E])
        region = sb("region", [P, BT, E])
        y_row = sb("y_row", [P, 2, TT], U32)
        tau = sb("tau", [P, TAB])
        filler = sb("filler", [P, SPARE * TH, ROW])
        w_in = sb("w_in", [P, D])
        wT = sb("wT", [P, D + 1])
        wr = sb("wr", [P, 1])
        wr_rep = sb("wr_rep", [P, P])
        wg = sb("wg", [P, E])
        bg_rep = sb("bg_rep", [P, E])
        b1_in = sb("b1_in", [E * C + 2, P])
        b1T = sb("b1T", [P, E * C + 2])
        b2_rep = sb("b2_rep", [P, E * D])
        wf = sb("wf", [P, 2 * E * H])
        w1f, w2f = wf[:, 0:E * H], wf[:, E * H:2 * E * H]
        w1h = sb("w1h", [P, E * H], F16)
        w1l = sb("w1l", [P, E * H], F16)
        w2h = sb("w2h", [P, E * H], F16)
        w2l = sb("w2l", [P, E * H], F16)
        wmax = sb("wmax", [P, 4])
        wmax_all = sb("wmax_all", [P, 4])
        pow2 = sb("pow2", [P, 4], I32)
        scale = sb("scale", [P, 4])
        inv = sb("inv", [P, 4])
        X = sb("X", [P, TT, D])
        adj_sb = sb("adj_sb", [P, BT, N], I32)
        S = sb("S", [P, BT, N])
        xn = sb("xn", [P, BT, D])
        xn2 = sb("xn2", [P, BT, D])
        stats = sb("stats", [P, 2, BT, 6])
        mv = sb("mv", [P, 2, BT, 2])
        rstd = sb("rstd", [P, 2, BT])
        newton = sb("newton", [P, 2, BT])
        shift = sb("shift", [P, 2, BT])
        xnT = sb("xnT", [P, G, N])
        xn2T = sb("xn2T", [P, G, N])
        h_sb = sb("h_sb", [P, G, GT, D + 1])
        pT = sb("pT", [P, G, 2 * N])
        rmax = sb("rmax", [P, BT])
        nsum = sb("nsum", [P, BT])
        negm = sb("negm", [P, BT])
        psum_p = sb("psum_p", [P, BT])
        rsum = sb("rsum", [P, BT])
        packs = [sb("pack", [P, 2, BT, ROW]), sb("pack_late", [P, 2, BT, ROW])]
        lg = sb("lg", [P, BT, E])
        tmp = sb("tmp", [P, BT, E])
        oh1 = sb("oh1", [P, BT, E])
        oh2 = sb("oh2", [P, BT, E])
        picks = sb("picks", [P, BT, E], BF16)
        picks_before = sb("picks_before", [P, E])
        picks_sum = sb("picks_sum", [P, E])
        picks_before16 = sb("picks_before16", [P, E], BF16)
        m1 = sb("m1", [P, BT])
        m2 = sb("m2", [P, BT])
        f1 = sb("f1", [P, BT])
        f2 = sb("f2", [P, BT])
        slot = sb("slot", [P, BT, E])
        target_f = sb("target_f", [P, 2, BT])
        targets = [sb("target", [P, 2, BT], U32), sb("target_late", [P, 2, BT], U32)]
        gap = sb("gap", [P, TT])
        wts = sb("wts", [P, 2, TT])
        cnt = sb("cnt", [P, E])
        cnt_i = sb("cnt_i", [P, E], I32)
        tiles = sb("tiles", [P, E])
        cum = sb("cum", [P, 4, E])
        done = sb("done", [P, TAB, E])
        donec = sb("donec", [P, TAB, E])
        tab_e = sb("tab_e", [P, TAB])
        tab_k = sb("tab_k", [P, TAB])
        tab_row = sb("tab_row", [P, TAB])
        expert_of = sb("expert_of", [P, TAB], I32)
        row_of = sb("row_of", [P, TAB], I32)
        fill_row = sb("fill_row", [P, E], I32)
        XL = sb("XL", [P, XS, TH, ROW])
        xT = sb("xT", [P, 2, 2 * T], F16)
        hid = S[:, :, :].rearrange("p (k c) n -> p k (c n)", k=2)
        hh = adj_sb[:, :, :].bitcast(F16).rearrange("p (k c) n -> p k (c n)", k=4)
        hl = sb("hl", [P, 4, C * T], F16)
        y_sb = sb("y_sb", [P, 4, T])
        yf = wf[:, :].rearrange("p (s c t d) -> p s c t d", s=YS, c=2, t=FT)

        s_const = sem("s_const")
        s_wl = sem("s_wl")
        s_w1 = sem("s_w1")
        s_w2 = sem("s_w2")
        s_filled = sem("s_filled")
        s_x = sem("s_x")
        s_adj = sem("s_adj")
        s_prep_ps = sem("s_prep_ps")
        s_prep = sem("s_prep")
        s_amax = sem("s_amax")
        s_gmax = sem("s_gmax")
        s_scale = sem("s_scale")
        s_whi = sem("s_whi")
        s_wsc = sem("s_wsc")
        s_wlo = sem("s_wlo")
        s_rstd = sem("s_rstd")
        s_xn = sem("s_xn")
        s_t1 = sem("s_t1")
        s_ts1 = sem("s_ts1")
        s_hr = sem("s_hr")
        s_h = sem("s_h")
        s_mask = sem("s_mask")
        s_s = sem("s_s")
        s_negm = sem("s_negm")
        s_sum = sem("s_sum")
        s_leaky = sem("s_leaky")
        s_p = sem("s_p")
        s_pt = sem("s_pt")
        s_pts = sem("s_pts")
        s_av = sem("s_av")
        s_x1 = sem("s_x1")
        s_rstd2 = sem("s_rstd2")
        s_xn2 = [sem("s_xn2_0"), sem("s_xn2_1")]
        s_t2 = sem("s_t2")
        s_ts2 = sem("s_ts2")
        s_lg = sem("s_lg")
        s_picks = sem("s_picks")
        s_rank = sem("s_rank")
        s_phi = sem("s_phi")
        s_pack = sem("s_pack")
        s_pack2 = sem("s_pack2")
        s_turn = sem("s_turn")
        s_scat = sem("s_scat")
        s_packfree = sem("s_packfree")
        s_egap = sem("s_egap")
        s_cnt = sem("s_cnt")
        s_tab = sem("s_tab")
        s_load = [sem(f"s_load{i}") for i in range(XS)]
        s_tt = sem("s_tt")
        s_tts = sem("s_tts")
        s_z = sem("s_z")
        s_g = sem("s_g")
        s_hi = sem("s_hi")
        s_split = sem("s_split")
        s_y = sem("s_y")
        s_ys = sem("s_ys")
        s_ysc = [sem(f"s_ysc{i}") for i in range(4)]
        s_yl = [sem(f"s_yl{i}") for i in range(YS)]
        s_fin0 = sem("s_fin0")
        s_fin = sem("s_fin")
        s_out = sem("s_out")
        s_vturn = sem("s_vturn")
        s_aturn = sem("s_aturn")
        s_sturn = sem("s_sturn")
        s_v = sem("s_v")
        s_vn = sem("s_vn")
        s_va = sem("s_va")
        s_vr = sem("s_vr")
        s_vt = sem("s_vt")

        T_BANK = bank[0]
        HB = [bank[1], bank[2]]
        PT = [bank[3], bank[4]]
        AR = [bank[5], bank[6]]
        MISC = bank[7]
        LOGITS = MISC[:, 64:64 + BT * E]
        RANK = MISC[:, 128:128 + BT * E]
        COUNT = MISC[:, 192:192 + E]
        TB = [bank[0], bank[7]]
        Z = [[bank[1], bank[2]], [bank[3], bank[4]]]
        Y = [bank[5], bank[6]]

        def experts(eng, s, n):
            return nc.values_load_multi_w_load_instructions(
                expert_of[0:1, bass.ds(s, n)], [eng.engine], min_val=0, max_val=E - 1,
                skip_runtime_bounds_check_because="the tile table is cut off at E - 1")[1]

        block = ctx.enter_context(nc.Block())

        @block.sync
        def _(sp):
            def load_x(b):
                sp.dma_start(X[:, bass.ds(b * BT, BT), :], x_v[:, bass.ds(b * BT, BT), :]).then_inc(s_x, 16)

            def load_adj(b):
                sp.dma_start(adj_sb[:, :, :], adj_v[:, bass.ds(b * BT, BT), :]).then_inc(s_adj, 16)

            load_x(0)
            for dst, src in ((w_in[:, :], W), (wg[:, :], Wg),
                             (b1_in[0:E * C, :], b1.rearrange("e (c p) -> (e c) p", p=P))):
                sp.dma_start(dst, src).then_inc(s_wl, 16)
            load_adj(0)
            sp.wait_ge(s_x, 16)
            load_x(1)
            sp.dma_start(w1f[:, :].rearrange("p (e h) -> p e h", e=E), W1.rearrange("e d h -> d e h")
                         ).then_inc(s_w1, 16)
            sp.dma_start(w2f[:, :].rearrange("p (k d) -> p k d", d=D), W2.rearrange("e (c p) d -> p (e c) d", p=P)
                         ).then_inc(s_w2, 16)
            sp.wait_ge(s_const, 2)
            sp.dma_start(rows_d[E * RS:E * RS + SPARE * T, :].rearrange("(h p) r -> p h r", p=P),
                         filler[:, :, :]).then_inc(s_filled, 16)
            with sp.Fori(1, NB - 1) as b:
                sp.wait_ge(s_x, b * 16 + 16)
                load_x(b + 1)
                sp.wait_ge(s_mask, b * G)
                load_adj(b)
            sp.wait_ge(s_mask, (NB - 1) * G)
            load_adj(NB - 1)
            sp.wait_ge(s_tab, 1)
            for e in range(E):
                row = sp.value_load(fill_row[0:1, e:e + 1], min_val=0, max_val=E * RS)
                sp.dma_start(rows_d[bass.ds(row, T), :].rearrange("(h p) r -> p h r", p=P),
                             filler[:, 0:TH, :]).then_inc(s_filled, 16)
            sp.wait_ge(s_filled, 16 * (E + 1))
            sp.wait_ge(s_scat, 16 * 2 * BT * NB)

            def load(s, k, wait):
                if wait is not None:
                    sp.wait_ge(s_ysc[k % 4], wait)
                    sp.sem_inc(s_sturn, 1)
                row = sp.value_load(row_of[0:1, bass.ds(s, 1)], min_val=0, max_val=E * RS + SPARE * T - T)
                sp.dma_start(XL[:, k, :, :], rows_d[bass.ds(row, T), :].rearrange("(h p) r -> p h r", p=P)
                             ).then_inc(s_load[k], 16)

            for k in range(XS):
                load(k, k, None)
            with sp.Fori(1, NT // XS) as r:
                for k in range(XS):
                    load(r * XS + k, k, r * (XS // 4 * 16 * TH) + (k // 4 + 1 - XS // 4) * 16 * TH)
            for s in range(NT // XS * XS, NT):
                load(s, s % XS, (s - XS) // 4 * (16 * TH) + 16 * TH)
            for k in range(4):
                sp.wait_ge(s_ysc[k], 16 * TH * len(range(k, NT, 4)))

            def load_y(q, k):
                for c in range(2):
                    sp.dma_start(yf[:, k, c, :, :], y_v[:, c, bass.ds(q * FT, FT), :]).then_inc(s_yl[k], 16)

            for k in range(YS):
                load_y(k, k)
            with sp.Fori(1, FC // YS) as r:
                for k in range(YS):
                    sp.wait_ge(s_fin, r * YS + (k + 1 - YS))
                    load_y(r * YS + k, k)

        @block.gpsimd
        def _(pool):
            pool.memset(ident[:, :], 0.0)
            pool.memset(ones[:, :], 1.0)
            pool.memset(picks_before[:, :], 0.0)
            pool.memset(filler[:, :, 0:D], 0.0)
            pool.iota(filler[:, :, D:D + 1].bitcast(U32), pattern=[[0, SPARE * TH], [0, 1]], base=FAR,
                      channel_multiplier=0).then_inc(s_const, 1)
            pool.wait_ge(s_const, 1)
            pool.affine_select(out=ident[:, :], in_=ident[:, :], compare_op=ALU.not_equal, fill=1.0, base=0,
                               pattern=[[-1, P]], channel_multiplier=1)
            pool.affine_select(out=before[:, :], in_=ones[:, :], compare_op=ALU.is_gt, fill=0.0, base=0,
                               pattern=[[1, P]], channel_multiplier=-1)
            pool.iota(ramp[:, :, :], pattern=[[0, BT], [-1, E]], base=E, channel_multiplier=0,
                      allow_small_or_imprecise_dtypes=True)
            pool.iota(region[:, :, :], pattern=[[0, BT], [RS, E]], base=0, channel_multiplier=0,
                      allow_small_or_imprecise_dtypes=True)
            pool.iota(y_row[:, :, :], pattern=[[TOK, 2], [P, TT]], base=0, channel_multiplier=1)
            pool.iota(tau[:, :], pattern=[[1, TAB]], base=0, channel_multiplier=0,
                      allow_small_or_imprecise_dtypes=True).then_inc(s_const, 1)
            pool.wait_ge(s_amax, 1)
            pool.partition_all_reduce(wmax_all[:, :], wmax[:, :], P, RMAX).then_inc(s_gmax, 1)
            def scatter(b, late, c, ready):
                pool.wait_ge(ready, b + 1)
                pool.sem_inc(s_turn, 1)
                for t in range(BT):
                    pool.indirect_dma_start(
                        rows_d[:, :], bass.IndirectOffsetOnAxis(ap=targets[late][:, c, t:t + 1], axis=0),
                        packs[late][:, c, t, :], None).then_inc(s_scat, 16)

            def low_weights(b):
                pool.wait_ge(s_wsc, b + 1)
                pool.sem_inc(s_turn, 1)
                for n, (full, hi, lo) in enumerate(((w1f, w1h, w1l), (w2f, w2h, w2l))):
                    at = bass.ds(b * H, H)
                    last = pool.tensor_tensor(lo[:, at], full[:, at], hi[:, at], ALU.subtract)
                last.then_inc(s_wlo, 1)

            with pool.Fori(0, NB - 2) as b:
                scatter(b, 0, 0, s_pack)
                low_weights(b)
                scatter(b, 0, 1, s_pack2)
                pool.wait_ge(s_scat, b * (16 * 2 * BT) + 16 * 2 * BT)
                pool.sem_inc(s_packfree, 1)
            for b, late in ((NB - 2, 1), (NB - 1, 0)):
                scatter(b, late, 0, s_pack)
                scatter(b, late, 1, s_pack2)
            low_weights(NB - 2)
            low_weights(NB - 1)
            def scatter_back(s, k):
                pool.wait_ge(s_ys, s + 1)
                pool.sem_inc(s_turn, 1)
                for half in range(TH):
                    pool.indirect_dma_start(
                        y_d[:, :],
                        bass.IndirectOffsetOnAxis(ap=XL[:, k, half, D:D + 1].bitcast(U32), axis=0),
                        y_sb[:, k % 4, half * P:(half + 1) * P], None,
                        bounds_check=2 * TOK - 1, oob_is_err=False).then_inc(s_ysc[k % 4], 16)

            with pool.Fori(0, NT // XS) as r:
                for k in range(XS):
                    scatter_back(r * XS + k, k)
            for s in range(NT // XS * XS, NT):
                scatter_back(s, s % XS)

        @block.scalar
        def _(act):
            act.dma_start(b1_in[E * C:, :], a.rearrange("o (s p) -> (o s) p", p=P)).then_inc(s_wl, 16)
            act.dma_start(bg_rep[:, :], bg.rearrange("(o e) -> o e", o=1).broadcast_to([P, E])).then_inc(s_wl, 16)
            act.dma_start(b2_rep[:, :], b2.rearrange("(o e) d -> o (e d)", o=1).broadcast_to([P, E * D])
                          ).then_inc(s_wl, 16)
            def normalise(b, q):
                act.wait_ge(s_rstd, b + 1)
                act.sem_inc(s_aturn, 1)
                for t in range(q * 2 * GT, (q + 1) * 2 * GT):
                    last = act.activation(xn[:, t, :], X[:, bass.ds(b * BT + t, 1), :], ACT.Identity,
                                          bias=shift[:, 0, t:t + 1], scale=rstd[:, 0, t:t + 1])
                last.then_inc(s_xn, 1)

            def turned_first(i, q):
                act.wait_ge(s_t1, i * Q + (q + 1))
                act.activation(xnT[:, 2 * q:2 * q + 2, :], T_BANK[:, :].rearrange("p (g n) -> p g n", g=2), ACT.Copy
                               ).then_inc(s_ts1, 1)

            def turned_probs(j, g):
                act.wait_ge(s_pt, j * G + (g + 1))
                act.activation(pT[:, g, :], PT[g % 2][:, :], ACT.Copy).then_inc(s_pts, 1)

            def copy_h(i, g):
                act.wait_ge(s_hr, i * G + (g + 1))
                act.activation(h_sb[:, g, :, :], HB[g % 2][:, 0:GT * (D + 1)].rearrange("p (t d) -> p t d", t=GT),
                               ACT.Copy).then_inc(s_h, 1)

            def add_left(i):
                act.wait_ge(s_negm, i + 1)
                for g in range(G):
                    for t in range(g * GT, (g + 1) * GT):
                        last = act.activation(S[:, t, :], S[:, t, :], ACT.Identity,
                                              bias=h_sb[:, g, t % GT, D:])
                    last.then_inc(s_sum, 1)

            def probs(i, g):
                act.wait_ge(s_leaky, i * G + (g + 1))
                for t in range(g * GT, (g + 1) * GT):
                    last = act.activation(S[:, t, :], S[:, t, :], ACT.Exp, bias=negm[:, t:t + 1],
                                          accum_out=psum_p[:, t:t + 1])
                last.then_inc(s_p, 1)

            def turned_second(j, q):
                act.wait_ge(s_t2, j * Q + (q + 1))
                act.activation(xn2T[:, 2 * q:2 * q + 2, :], PT[q][:, :].rearrange("p (g n) -> p g n", g=2), ACT.Copy
                               ).then_inc(s_ts2, 1)

            def second_norm(j):
                act.wait_ge(s_rstd2, j + 1)
                act.sem_inc(s_aturn, 1)
                for t in range(2 * GT, BT):
                    last = act.activation(xn2[:, t, :], X[:, bass.ds(j * BT + t, 1), :], ACT.Identity,
                                          bias=shift[:, 1, t:t + 1], scale=rstd[:, 1, t:t + 1])
                last.then_inc(s_xn2[1], 1)

            def second_pack(j, late=0):
                pack = packs[late]
                act.wait_ge(s_pack, j + 1)
                act.activation(pack[:, 1, :, 0:D], pack[:, 0, :, 0:D], ACT.Copy).then_inc(s_pack2, 1)

            def high_rows(l, late=0, free=None):
                pack = packs[late]
                if free is not None:
                    act.wait_ge(s_packfree, free)
                for made in s_xn2:
                    act.wait_ge(made, l + 1)
                act.activation(pack[:, 0, :, 0:D // 2].bitcast(F16), xn2[:, :, :], ACT.Copy, scale=X_SCALE
                               ).then_inc(s_phi, 1)

            def high_weights(e):
                for n, (full, hi) in enumerate(((w1f, w1h), (w2f, w2h))):
                    last = act.activation(hi[:, bass.ds(e * H, H)], full[:, bass.ds(e * H, H)], ACT.Copy,
                                          scale=scale[:, n:n + 1])
                last.then_inc(s_whi, 1)

            def scaled_weights(e):
                act.wait_ge(s_whi, e + 1)
                act.sem_inc(s_aturn, 1)
                for n, full in enumerate((w1f, w2f)):
                    last = act.activation(full[:, bass.ds(e * H, H)], full[:, bass.ds(e * H, H)], ACT.Copy,
                                          scale=scale[:, n:n + 1])
                last.then_inc(s_wsc, 1)

            def batch(i, j, l, more, late=0):
                if i is not None:
                    copy_h(i, 0)
                    copy_h(i, 1)
                if l is not None:
                    turned_second(l, 1)
                if more:
                    normalise(i + 1, 0)
                    normalise(i + 1, 1)
                if j is not None:
                    high_weights(j)
                if more:
                    turned_first(i + 1, 0)
                if i is not None:
                    copy_h(i, 2)
                if l is not None:
                    high_rows(l, late, l + 1 if not late else None)
                if i is not None:
                    copy_h(i, 3)
                if more:
                    turned_first(i + 1, 1)
                if j is not None:
                    scaled_weights(j)
                if i is not None:
                    add_left(i)
                    if l is not None:
                        second_pack(l, late)
                    for g in range(G):
                        probs(i, g)
                        if g >= 1:
                            turned_probs(i, g - 1)
                    turned_probs(i, 3)
                if l is not None and i is None:
                    second_pack(l, late)
                if j is not None:
                    if more:
                        second_norm(j)
                    turned_second(j, 0)
                    if i is None:
                        turned_second(j, 1)

            act.wait_ge(s_const, 1)
            act.activation(psum_p[:, 0:1], ones[:, 0:1], ACT.Exp)
            normalise(0, 0)
            normalise(0, 1)
            turned_first(0, 0)
            turned_first(0, 1)
            batch(0, None, None, True)
            act.wait_ge(s_scale, 1)
            batch(1, 0, None, True)
            with act.Fori(2, NB - 1) as i:
                batch(i, i - 1, i - 2, True)
            batch(NB - 1, NB - 2, NB - 3, False)
            batch(None, NB - 1, NB - 2, False, 1)
            high_rows(NB - 1, 0, NB - 1)
            second_pack(NB - 1)
            act.activation(gap[:, :], gap[:, :], ACT.Exp).then_inc(s_egap, 1)
            act.activation(psum_p[:, 0:1], inv[:, 0:1], ACT.Gelu)

            act.wait_ge(s_tab, 1)

            def turned_tile(s, k):
                act.wait_ge(s_tt, s + 1)
                act.activation(xT[:, k % 2, :], TB[k % 2][:, 0:T].bitcast(F16), ACT.Copy).then_inc(s_tts, 1)

            def gelu(s, k, e, wait):
                k %= 2
                for c in range(C):
                    if c % 2 == 0:
                        act.wait_ge(s_z, s * 2 + (c // 2 + 1))
                        if wait:
                            act.wait_ge(s_split, s * 2 + (c // 2 - 3))
                        act.sem_inc(s_aturn, 1)
                    ins = act.activation(hid[:, k, c * T:(c + 1) * T], Z[k][c // 2][:, (c % 2) * T:(c % 2 + 1) * T],
                                         ACT.Gelu, bias=b1T[:, bass.ds(e * C + c, 1)], scale=inv[:, 0:1])
                    if c % 2 == 1:
                        ins.then_inc(s_g, 1)

            def tiles_of(s0, wait, n=4, last=False):
                es = experts(act, s0, n)
                for k in range(n):
                    if not (last and k == n - 1):
                        turned_tile(s0 + (k + 1), k + 1)
                    gelu(s0 + k, k, es[k], wait or k >= 2)

            turned_tile(0, 0)
            tiles_of(0, False)
            with act.Fori(1, NT // 4) as r:
                tiles_of(r * 4, True)
            tiles_of(NT // 4 * 4, True, NT % 4, last=True)

            with act.Fori(0, FC) as q:
                act.wait_ge(s_fin, q + 1)
                act.dma_start(out_v[:, bass.ds(q * FT, FT), :], X[:, bass.ds(q * FT, FT), :]).then_inc(s_out, 16)
            act.wait_ge(s_out, 16 * FC)

        @block.tensor
        def _(pe):
            pe.wait_ge(s_const, 2)
            pe.wait_ge(s_wl, 16 * 6)
            pe.transpose(T_BANK[:, 0:D], w_in[:, :], ident[:, :])
            pe.transpose(T_BANK[:, 256:256 + E * C + 2], b1_in[:, :], ident[0:E * C + 2, 0:E * C + 2]
                         ).then_inc(s_prep_ps, 1)
            pe.wait_ge(s_prep, 1)
            pe.matmul(T_BANK[:, 128:130], w_in[:, :], b1T[:, E * C:], start=True, stop=True).then_inc(s_prep_ps, 1)
            pe.wait_ge(s_prep, 2)

            def turn_first(i, q):
                pe.wait_ge(s_xn, i * Q + (q + 1))
                if q:
                    pe.wait_ge(s_ts1, i * Q + q)
                for t in range(2 * GT):
                    last = pe.transpose(T_BANK[:, t * P:(t + 1) * P], xn[:, q * 2 * GT + t, :], ident[:, :])
                last.then_inc(s_t1, 1)

            def project(i, g, first):
                pe.wait_ge(s_ts1, i * Q + (g // 2 + 1))
                if g >= 2:
                    pe.wait_ge(s_h, i * G + (g - 1))
                for t in range(GT):
                    pe.matmul(HB[g % 2][:, t * (D + 1):(t + 1) * (D + 1)], xnT[:, g, t * P:(t + 1) * P], wT[:, :],
                              start=True, stop=True)
                if first:
                    if g >= 2:
                        pe.wait_ge(s_s, i * G + (g - 1))
                else:
                    pe.wait_ge(s_x1, (i - 1) * G + (g + 1))
                pe.matmul(AR[g % 2][:, N:2 * N], wr_rep[:, :], xnT[:, g, :], start=True, stop=True
                          ).then_inc(s_hr, 1)

            def turn_probs(j, g):
                pe.wait_ge(s_p, j * G + (g + 1))
                if g >= 2:
                    pe.wait_ge(s_pts, j * G + (g - 1))
                for n in range(GT):
                    for t in range(GT):
                        last = pe.transpose(PT[g % 2][:, n * N + t * P:n * N + (t + 1) * P],
                                            S[:, g * GT + t, n * P:(n + 1) * P], ident[:, :])
                last.then_inc(s_pt, 1)

            def attend(j, g, scores):
                pe.wait_ge(s_pts, j * G + (g + 1))
                pe.wait_ge(s_s, scores)
                for t in range(GT):
                    for n in range(GT):
                        last = pe.matmul(AR[g % 2][:, t * P:(t + 1) * P],
                                         pT[:, g, n * N + t * P:n * N + (t + 1) * P],
                                         h_sb[:, g, n, 0:D], start=(n == 0), stop=(n == GT - 1))
                last.then_inc(s_av, 1)

            def turn_second(j, q, more):
                pe.wait_ge(s_xn2[q], j + 1)
                pe.wait_ge(s_pts, (j + 1) * G + (q + 3 if more else 0))
                for t in range(2 * GT):
                    last = pe.transpose(PT[q][:, t * P:(t + 1) * P], xn2[:, q * 2 * GT + t, :], ident[:, :])
                last.then_inc(s_t2, 1)

            def route(j, g):
                pe.wait_ge(s_ts2, j * Q + (g // 2 + 1))
                for t in range(GT):
                    n = (g * GT + t) * E
                    last = pe.matmul(LOGITS[:, n:n + E], xn2T[:, g, t * P:(t + 1) * P], wg[:, :], start=True, stop=True)
                if g == G - 1:
                    last.then_inc(s_lg, 1)

            def rank(j):
                pe.wait_ge(s_picks, j + 1)
                flat = picks[:, :, :].rearrange("p t e -> p (t e)")
                pe.matmul(RANK[:, :], before16[:, :], flat, start=True, stop=False)
                for t in range(1, BT):
                    pe.matmul(RANK[:, t * E:], ones16[:, :], flat[:, 0:(BT - t) * E], start=False, stop=False)
                pe.matmul(RANK[:, :].rearrange("p (t e) -> p t e", e=E), ones16[:, :],
                          picks_before16[:, :].rearrange("p (o e) -> p o e", o=1).broadcast_to([P, BT, E]),
                          start=False, stop=True).then_inc(s_rank, 1)

            def batch(i, j, l, more):
                if i is not None:
                    project(i, 0, j is None)
                    project(i, 1, j is None)
                if l is not None:
                    turn_second(l, 1, True)
                    for g in range(G):
                        route(l, g)
                if j is not None:
                    for g in range(2, G):
                        if i is None:
                            pe.wait_ge(s_x1, j * G + (g - 1))
                        attend(j, g, (j + 1) * G + ((g - 1) if i is not None else 0))
                if more:
                    turn_first(i + 1, 0)
                if i is not None:
                    project(i, 2, j is None)
                if l is not None:
                    rank(l)
                if i is not None:
                    project(i, 3, j is None)
                if more:
                    turn_first(i + 1, 1)
                if i is not None:
                    turn_probs(i, 0)
                    turn_probs(i, 1)
                    for g in range(2):
                        attend(i, g, i * G + (g + 3))
                        turn_probs(i, g + 2)
                if j is not None:
                    turn_second(j, 0, i is not None)

            turn_first(0, 0)
            turn_first(0, 1)
            batch(0, None, None, True)
            batch(1, 0, None, True)
            with pe.Fori(2, NB - 1) as i:
                batch(i, i - 1, i - 2, True)
            batch(NB - 1, NB - 2, NB - 3, False)
            batch(None, NB - 1, NB - 2, False)
            turn_second(NB - 1, 1, False)
            for g in range(G):
                route(NB - 1, g)
            rank(NB - 1)
            pe.wait_ge(s_pack, NB)
            pe.matmul(COUNT, ones16[:, :], picks_before16[:, :], start=True, stop=True).then_inc(s_cnt, 1)

            pe.wait_ge(s_tab, 1)
            pe.wait_ge(s_wlo, E)

            def turn_tile(s, k, landed):
                pe.wait_ge(s_load[k], landed)
                parts = XL[:, k, :, :].bitcast(F16)
                tb = TB[k % 2][:, 0:T].bitcast(F16)
                for part in range(2):
                    for half in range(TH):
                        last = pe.transpose(tb[:, part * T + half * P:part * T + (half + 1) * P],
                                            parts[:, half, part * D:(part + 1) * D], ident16[:, :])
                last.then_inc(s_tt, 1)

            def hidden(s, k, e, wait):
                k %= 2
                pe.wait_ge(s_tts, s + 1)
                for c in range(C):
                    if wait and c % 2 == 0:
                        pe.wait_ge(s_g, s * 2 + (c // 2 - 3))
                    z = Z[k][c // 2][:, (c % 2) * T:(c % 2 + 1) * T]
                    hi = w1h[:, bass.ds(e * H + c * P, P)]
                    lo = w1l[:, bass.ds(e * H + c * P, P)]
                    pe.matmul(z, hi, xT[:, k, 0:T], start=True, stop=False)
                    pe.matmul(z, hi, xT[:, k, T:2 * T], start=False, stop=False)
                    last = pe.matmul(z, lo, xT[:, k, 0:T], start=False, stop=True)
                    if c % 2 == 1:
                        last.then_inc(s_z, 1)

            def output(u, k, e, wait):
                pe.wait_ge(s_split, u * 2 + 1)
                if wait:
                    pe.wait_ge(s_ys, u - 1)
                for half in range(TH):
                    y = Y[k % 2][:, half * P:(half + 1) * P]
                    for c in range(C):
                        if half == 0 and c == 2:
                            pe.wait_ge(s_split, u * 2 + 2)
                        at = slice(c * T + half * P, c * T + (half + 1) * P)
                        hi = w2h[:, bass.ds(e * H + c * P, P)]
                        lo = w2l[:, bass.ds(e * H + c * P, P)]
                        pe.matmul(y, hh[:, k % 4, at], hi, start=(c == 0), stop=False)
                        pe.matmul(y, hh[:, k % 4, at], lo, start=False, stop=False)
                        last = pe.matmul(y, hl[:, k % 4, at], hi, start=False, stop=(c == C - 1))
                last.then_inc(s_y, 1)

            turn_tile(0, 0, 16)
            es = experts(pe, 0, XS)
            for s in range(XS):
                if s >= LAG:
                    output(s - LAG, s - LAG, es[s - LAG], s - LAG >= 2)
                turn_tile(s + 1, (s + 1) % XS, 16 * ((s + 1) // XS + 1))
                hidden(s, s, es[s], s >= 2)

            def tiles_of(r, s0, n=XS, last=False):
                for k in range(n):
                    if k % 4 == 0:
                        es = experts(pe, s0 + k - LAG, 4 + LAG)
                    output(s0 + (k - LAG), k - LAG + XS, es[k % 4], True)
                    if not (last and k == n - 1):
                        turn_tile(s0 + (k + 1), (k + 1) % XS, r * 16 + 16 * ((k + 1) // XS + 1))
                    hidden(s0 + k, k, es[k % 4 + LAG], True)

            with pe.Fori(1, NT // XS) as r:
                tiles_of(r, r * XS)
            tiles_of(NT // XS, NT // XS * XS, NT % XS, last=True)
            es = experts(pe, NT - LAG, LAG)
            for k in range(LAG):
                output(NT - LAG + k, (NT - LAG + k) % XS, es[k], True)

        @block.vector
        def _(dve):
            count = [0]

            def link(ins, sem_, base=0):
                count[0] += 1
                ins.then_inc(sem_, 1)
                dve.wait_ge(sem_, base + count[0])

            dve.sem_inc(s_packfree, 1)

            class Own:
                def __init__(self, sem_, each):
                    self.sem, self.each = sem_, each

                def begin(self, start):
                    self.start, self.n = start, 0

                def __call__(self, ins):
                    self.n += 1
                    ins.then_inc(self.sem, 1)
                    dve.wait_ge(self.sem, self.start + self.n)

                def beside(self, ins, b, t):
                    self.n += 1
                    ins.then_inc(self.sem, 1)
                    if b is not None:
                        dve.bn_stats(stats[:, 0, t, :], X[:, bass.ds(b * BT + t, 1), :])
                    dve.wait_ge(self.sem, self.start + self.n)

                def end(self):
                    assert self.n == self.each, self.n

            NORM, ATT, ROUT = 15, 2, 17
            norm, att, rout = Own(s_vn, NORM), Own(s_va, ATT), Own(s_vr, ROUT)

            def statistics(which, b):
                for t in range(BT):
                    last = dve.bn_stats(stats[:, which, t, :], X[:, bass.ds(b * BT + t, 1), :])
                return last

            def factors(which, last):
                norm(last)
                dve.sem_inc(s_vturn, 1)
                for w in which:
                    for t in range(BT):
                        last = dve.bn_aggr(mv[:, w, t, :], stats[:, w, t, :])
                norm(last)
                at = slice(which[0], which[-1] + 1)
                var, r, n = mv[:, at, :, 1], rstd[:, at, :], newton[:, at, :]
                norm(dve.tensor_scalar(var, var, EPS, float(1 << 26), ALU.add, ALU.mult))
                norm(dve.tensor_scalar(r.bitcast(I32), var.bitcast(I32), 1, None, ALU.logical_shift_right))
                norm(dve.tensor_scalar(r.bitcast(I32), r.bitcast(I32), -1.0, float(0x5F3759DF), ALU.mult, ALU.add))
                for grown in (1.0, 2.0, 16.0):
                    norm(dve.tensor_tensor(n, r, var, ALU.mult))
                    norm(dve.tensor_tensor(n, n, r, ALU.mult))
                    norm(dve.scalar_tensor_tensor(r, n, 3.0 * grown * grown, r, ALU.subtract, ALU.mult,
                                                  reverse0=True))
                norm(dve.scalar_tensor_tensor(shift[:, at, :], mv[:, at, :, 0], -1.0, r, ALU.mult, ALU.mult))
                for w in which:
                    dve.sem_inc((s_rstd, s_rstd2)[w], 1)

            def mask(i, j, g):
                if g == 0:
                    dve.wait_ge(s_adj, i * 16 + 16)
                if j is not None:
                    dve.wait_ge(s_pt, j * G + (g + 1))
                at = slice(g * GT, (g + 1) * GT)
                dve.tensor_scalar(S[:, at, :], adj_sb[:, at, :], 0.0, MASKED, ALU.is_equal, ALU.mult
                                  ).then_inc(s_mask, 1)

            def right_scores(i, g):
                dve.wait_ge(s_mask, i * G + (g + 1))
                dve.wait_ge(s_hr, i * G + (g + 1))
                dve.sem_inc(s_vturn, 1)
                for t in range(g * GT, (g + 1) * GT):
                    last = dve.tensor_tensor_reduce(S[:, t, :], S[:, t, :], AR[g % 2][:, N:2 * N], 1.0, -3e38,
                                                    ALU.add, ALU.max, rmax[:, t:t + 1])
                last.then_inc(s_s, 1)

            def row_maxima(i):
                left = h_sb[:, :, :, D].rearrange("p g t -> p (g t)")
                dve.wait_ge(s_s, i * G + G)
                dve.wait_ge(s_h, i * G + G)
                att(dve.scalar_tensor_tensor(nsum[:, :], rmax[:, :], -1.0, left, ALU.mult, ALU.subtract))
                dve.scalar_tensor_tensor(negm[:, :], nsum[:, :], SLOPE, nsum[:, :], ALU.mult, ALU.min
                                         ).then_inc(s_negm, 1)

            def leaky(i, g):
                dve.wait_ge(s_sum, i * G + (g + 1))
                both = S[:, g * GT:(g + 1) * GT, :]
                dve.scalar_tensor_tensor(both, both, SLOPE, both, ALU.mult, ALU.max).then_inc(s_leaky, 1)

            def residual(j, g):
                dve.wait_ge(s_av, j * G + (g + 1))
                for t in range(g * GT, (g + 1) * GT):
                    xt = X[:, bass.ds(j * BT + t, 1), :].rearrange("p o d -> p (o d)")
                    last = dve.scalar_tensor_tensor(xt, AR[g % 2][:, (t % GT) * P:(t % GT + 1) * P],
                                                    rsum[:, t:t + 1], xt, ALU.mult, ALU.add)
                last.then_inc(s_x1, 1)

            def second_norm(j, shared):
                for t in range(2 * GT if shared else BT):
                    last = dve.tensor_scalar(xn2[:, t, :], X[:, bass.ds(j * BT + t, 1), :], mv[:, 1, t, 0:1],
                                             rstd[:, 1, t:t + 1], ALU.subtract, ALU.mult)
                    if t == 2 * GT - 1 or t == BT - 1:
                        last.then_inc(s_xn2[t // (2 * GT)], 1)

            def over_e(v):
                return v[:, :].rearrange("p (t o) -> p t o", o=1).broadcast_to([P, BT, E])

            def choose(oh, m, f, b, t):
                rout.beside(dve.tensor_reduce(m[:, :], lg[:, :, :], AX, ALU.max), b, t)
                rout.beside(dve.tensor_tensor(tmp[:, :, :], lg[:, :, :], over_e(m), ALU.is_equal), b, t + 1)
                rout.beside(dve.tensor_tensor(tmp[:, :, :], tmp[:, :, :], ramp[:, :, :], ALU.mult), b, t + 2)
                rout.beside(dve.tensor_reduce(f[:, :], tmp[:, :, :], AX, ALU.max), b, t + 3)
                rout(dve.tensor_tensor(oh[:, :, :], ramp[:, :, :], over_e(f), ALU.is_equal))

            def first_choice(l, b=None):
                if b is not None:
                    dve.wait_ge(s_x, b * 16 + 16)
                    dve.sem_inc(s_vturn, 1)
                    for t in range(4):
                        dve.bn_stats(stats[:, 0, t, :], X[:, bass.ds(b * BT + t, 1), :])
                dve.wait_ge(s_lg, l + 1)
                rout(dve.tensor_tensor(lg[:, :, :], LOGITS.rearrange("p (t e) -> p t e", e=E),
                                       bg_rep[:, :].rearrange("p (o e) -> p o e", o=1).broadcast_to([P, BT, E]),
                                       ALU.add))
                choose(oh1, m1, f1, b, 4)

            def second_choice(l):
                rout(dve.scalar_tensor_tensor(lg[:, :, :], oh1[:, :, :], REJECT, lg[:, :, :], ALU.mult, ALU.add))
                choose(oh2, m2, f2, None, 0)
                dve.tensor_tensor(picks[:, :, :], oh1[:, :, :], oh2[:, :, :], ALU.add).then_inc(s_picks, 1)
                dve.tensor_tensor(gap[:, bass.ds(l * BT, BT)], m2[:, :], m1[:, :], ALU.subtract)

            def picks_total(l):
                dve.wait_ge(s_picks, l + 1)
                rout(dve.tensor_reduce(picks_sum[:, :], picks[:, :, :].rearrange("p t e -> p e t"), AX, ALU.add))
                rout(dve.tensor_tensor(picks_before[:, :], picks_before[:, :], picks_sum[:, :], ALU.add))

            def destinations(l):
                dve.wait_ge(s_rank, l + 1)
                dve.tensor_copy(picks_before16[:, :], picks_before[:, :])
                rout(dve.tensor_tensor(slot[:, :, :], RANK.rearrange("p (t e) -> p t e", e=E), region[:, :, :],
                                       ALU.add))
                dve.tensor_tensor(oh1[:, :, :], oh1[:, :, :], slot[:, :, :], ALU.mult)
                rout(dve.tensor_tensor(oh2[:, :, :], oh2[:, :, :], slot[:, :, :], ALU.mult))
                dve.tensor_reduce(target_f[:, 0, :], oh1[:, :, :], AX, ALU.add)
                rout(dve.tensor_reduce(target_f[:, 1, :], oh2[:, :, :], AX, ALU.add))

            def rows(l, late=0):
                pack, target = packs[late], targets[late]
                hi = pack[:, 0, :, 0:D // 2].bitcast(F16)
                lo = pack[:, 0, :, D // 2:D].bitcast(F16)
                dve.wait_ge(s_phi, l + 1)
                dve.scalar_tensor_tensor(lo, xn2[:, :, :], X_SCALE, hi, ALU.mult, ALU.subtract)
                dve.tensor_copy(pack[:, :, :, D].bitcast(U32), y_row[:, :, bass.ds(l * BT, BT)])
                dve.tensor_copy(target[:, :, :], target_f[:, :, :]).then_inc(s_pack, 1)

            def maximum(n, full, landed):
                dve.wait_ge(landed, 16)
                return dve.tensor_reduce(wmax[:, n:n + 1], full[:, :], AX, ALU.max, apply_absolute_value=True)

            def scales():
                dve.wait_ge(s_gmax, 1)
                link(dve.scalar_tensor_tensor(wmax_all[:, 2:3], wmax_all[:, 0:1], float(D), wmax_all[:, 2:3],
                                              ALU.mult, ALU.add), s_v)
                link(dve.tensor_scalar(wmax_all[:, :], wmax_all[:, :], 1e-12, None, ALU.max), s_v)
                link(dve.tensor_scalar(pow2[:, :], wmax_all[:, :].bitcast(I32), 0x7F800000, None, ALU.bitwise_and),
                     s_v)
                link(dve.tensor_scalar(scale[:, :].bitcast(I32), pow2[:, :], -1.0, float((254 + 13) << 23),
                                       ALU.mult, ALU.add), s_v)
                link(dve.tensor_scalar(inv[:, :].bitcast(I32), scale[:, :].bitcast(I32), -1.0, float(254 << 23),
                                       ALU.mult, ALU.add), s_v)
                dve.tensor_tensor(inv[:, 1:2], inv[:, 1:2], inv[:, 2:3], ALU.mult)
                dve.tensor_scalar(inv[:, 0:1], inv[:, 0:1], 1.0 / X_SCALE, None, ALU.mult).then_inc(s_scale, 1)

            def batch(i, j, l, more, late=0, weights=False, shared=True):
                if l is not None:
                    rout.begin(l * ROUT)
                if j is not None:
                    dve.wait_ge(s_p, j * G + G)
                    att(dve.reciprocal(rsum[:, :], psum_p[:, :]))
                    residual(j, 0)
                    residual(j, 1)
                if i is not None:
                    for g in range(G if l is None else 2):
                        mask(i, j, g)
                    if weights:
                        dve.wait_ge(s_x, 32)
                        last = statistics(0, 1)
                        dve.wait_ge(s_xn, Q)
                        factors([0], last)
                        norm.begin(2 * NORM)
                        link(dve.tensor_reduce(wmax[:, 2:3], b1T[:, 0:E * C], AX, ALU.max,
                                               apply_absolute_value=True), s_v)
                        dve.tensor_copy(wmax[:, 3:4], wmax[:, 2:3])
                        maximum(0, w1f, s_w1)
                    right_scores(i, 0)
                    right_scores(i, 1)
                    if l is not None:
                        mask(i, j, 2)
                        mask(i, j, 3)
                    if weights:
                        maximum(1, w2f, s_w2).then_inc(s_amax, 1)
                if l is not None:
                    first_choice(l, i + 2 if more else None)
                    second_choice(l)
                if j is not None:
                    residual(j, 2)
                    residual(j, 3)
                if l is not None:
                    picks_total(l)
                if i is not None:
                    right_scores(i, 2)
                    right_scores(i, 3)
                if l is not None:
                    destinations(l)
                if i is not None:
                    row_maxima(i)
                if more and l is None:
                    dve.wait_ge(s_x, i * 16 + 48)
                    dve.sem_inc(s_vturn, 1)
                    last = statistics(0, i + 2)
                if l is not None:
                    rows(l, late)
                if j is not None:
                    dve.wait_ge(s_x1, j * G + G)
                    dve.sem_inc(s_vturn, 1)
                    last = statistics(1, j)
                if i is not None:
                    for g in range(G):
                        leaky(i, g)
                if weights:
                    scales()
                if more:
                    dve.wait_ge(s_xn, i * Q + 2 * Q)
                if more or j is not None:
                    factors(([0] if more else []) + ([1] if j is not None else []), last)
                if j is not None:
                    second_norm(j, shared)

            norm.begin(0)
            dve.wait_ge(s_x, 16)
            factors([0], statistics(0, 0))
            dve.wait_ge(s_const, 2)
            dve.tensor_copy(ident16[:, :], ident[:, :])
            dve.tensor_copy(ones16[:, :], ones[:, :])
            dve.tensor_copy(before16[:, :], before[:, :])
            dve.memset(picks_before16[:, :], 0.0)
            dve.wait_ge(s_prep_ps, 1)
            dve.tensor_copy(wT[:, 0:D], T_BANK[:, 0:D])
            dve.tensor_copy(b1T[:, :], T_BANK[:, 256:256 + E * C + 2]).then_inc(s_prep, 1)
            dve.wait_ge(s_prep_ps, 2)
            dve.tensor_copy(wT[:, D:], T_BANK[:, 128:129])
            link(dve.tensor_copy(wr[:, :], T_BANK[:, 129:130]), s_v)
            dve.tensor_scalar(wr_rep[:, :], ones[:, :], wr[:, :], None, ALU.mult).then_inc(s_prep, 1)
            norm.begin(NORM), att.begin(0)
            batch(0, None, None, True, weights=True)
            norm.begin(3 * NORM), att.begin(ATT - 1)
            batch(1, 0, None, True)
            with dve.Fori(2, NB - 2) as i:
                norm.begin(i * NORM + 2 * NORM), att.begin(i * ATT - 1)
                batch(i, i - 1, i - 2, True)
                norm.end(), att.end(), rout.end()
            for i in (NB - 2, NB - 1):
                norm.begin(NB * NORM + (i + 2 - NB) * NORM), att.begin(i * ATT - 1)
                batch(i, i - 1, i - 2, False, shared=i < NB - 1)
            norm.begin(NB * NORM + 2 * NORM), att.begin(NB * ATT - 1)
            batch(None, NB - 1, NB - 2, False, 1, shared=False)
            rout.begin((NB - 1) * ROUT)
            first_choice(NB - 1)
            second_choice(NB - 1)
            picks_total(NB - 1)
            destinations(NB - 1)
            rows(NB - 1)

            count[0] = 0

            def lt(ins):
                link(ins, s_vt)

            dve.wait_ge(s_cnt, 1)
            lt(dve.tensor_copy(cnt[:, :], COUNT))
            lt(dve.tensor_scalar(cnt_i[:, :], cnt[:, :], float(T - 1), None, ALU.add))
            lt(dve.tensor_scalar(cnt_i[:, :], cnt_i[:, :], T.bit_length() - 1, None, ALU.arith_shift_right))
            lt(dve.tensor_copy(tiles[:, :], cnt_i[:, :]))
            lt(dve.tensor_copy(cum[:, 0, :], tiles[:, :]))
            for n, d in enumerate((1, 2, 4)):
                dve.tensor_copy(cum[:, n + 1, 0:d], cum[:, n, 0:d])
                lt(dve.tensor_tensor(cum[:, n + 1, d:E], cum[:, n, d:E], cum[:, n, 0:E - d], ALU.add))
            lt(dve.tensor_tensor(done[:, :, :], cum[:, 3, :].rearrange("p (o e) -> p o e", o=1).broadcast_to([P, TAB, E]),
                                 tau[:, :].rearrange("p (n o) -> p n o", o=1).broadcast_to([P, TAB, E]), ALU.is_le))
            lt(dve.tensor_reduce(tab_e[:, :], done[:, :, :], AX, ALU.add))
            lt(dve.tensor_tensor(donec[:, :, :], done[:, :, :],
                                 tiles[:, :].rearrange("p (o e) -> p o e", o=1).broadcast_to([P, TAB, E]), ALU.mult))
            lt(dve.tensor_reduce(tab_k[:, :], donec[:, :, :], AX, ALU.add))
            lt(dve.tensor_tensor(tab_k[:, :], tau[:, :], tab_k[:, :], ALU.subtract))
            lt(dve.tensor_scalar(tab_k[:, :], tab_k[:, :], float(T), None, ALU.mult))
            lt(dve.scalar_tensor_tensor(tab_row[:, :], tab_e[:, :], float(RS), tab_k[:, :], ALU.mult, ALU.add))
            dve.tensor_copy(row_of[:, :], tab_row[:, :])
            dve.tensor_scalar(expert_of[:, :], tab_e[:, :], float(E - 1), None, ALU.min)
            dve.tensor_tensor(fill_row[:, :], cnt[:, :], region[:, 0, :], ALU.add).then_inc(s_tab, 1)
            dve.wait_ge(s_egap, 1)
            lt(dve.tensor_scalar(wts[:, 1, :], gap[:, :], 1.0, None, ALU.add))
            lt(dve.reciprocal(wts[:, 0, :], wts[:, 1, :]))
            lt(dve.tensor_tensor(wts[:, 1, :], gap[:, :], wts[:, 0, :], ALU.mult))
            dve.wait_ge(s_tab, 1)

            def split(s, k):
                for half in range(2):
                    at = slice(half * 2 * T, (half + 1) * 2 * T)
                    dve.wait_ge(s_g, s * 2 + (half + 1))
                    dve.tensor_scalar(hh[:, k, at], hid[:, k % 2, at], scale[:, 2:3], None, ALU.mult
                                      ).then_inc(s_hi, 1)
                    dve.wait_ge(s_hi, s * 2 + (half + 1))
                    dve.scalar_tensor_tensor(hl[:, k, at], hid[:, k % 2, at], scale[:, 2:3], hh[:, k, at],
                                             ALU.mult, ALU.subtract).then_inc(s_split, 1)

            def outputs(u, k, e, scattered):
                dve.wait_ge(s_y, u + 1)
                if scattered is not None:
                    dve.wait_ge(s_ysc[k], scattered)
                both = [v.rearrange("p (h d) -> p h d", d=D) for v in (y_sb[:, k, :], Y[k % 2][:, 0:T])]
                bias = b2_rep[:, bass.ds(e * D, D)].rearrange("p (o d) -> p o d", o=1).broadcast_to([P, TH, D])
                dve.scalar_tensor_tensor(both[0], both[1], inv[:, 1:2], bias, ALU.mult, ALU.add).then_inc(s_ys, 1)

            es = experts(dve, 0, 4 - LAG)
            for s in range(4):
                if s >= LAG:
                    outputs(s - LAG, s - LAG, es[s - LAG], None)
                split(s, s)

            def tiles_of(s0, scattered, n=4):
                es = experts(dve, s0 - LAG, n)
                for k in range(n):
                    slot_ = (k - LAG) % 4
                    outputs(s0 + (k - LAG), slot_, es[k], scattered[slot_])
                    split(s0 + k, k)

            tiles_of(4, (16 * TH, None, None, None))
            with dve.Fori(2, NT // 4) as r:
                round_ = r * (16 * TH)
                tiles_of(r * 4, (round_,) + (round_ - 16 * TH,) * 3)
            round_ = NT // 4 * (16 * TH)
            tiles_of(NT // 4 * 4, (round_,) + (round_ - 16 * TH,) * 3, NT % 4)
            es = experts(dve, NT - LAG, LAG)
            for u in range(NT - LAG, NT):
                outputs(u, u % 4, es[u - NT + LAG], u // 4 * (16 * TH))

            def finish(q, k, loaded):
                dve.wait_ge(s_yl[k], loaded)
                for c, done_ in enumerate((s_fin0, s_fin)):
                    if c:
                        dve.wait_ge(s_fin0, q + 1)
                    for t in range(FT):
                        xt = X[:, bass.ds(q * FT + t, 1), :].rearrange("p o d -> p (o d)")
                        last = dve.scalar_tensor_tensor(xt, yf[:, k, c, t, :], wts[:, c, bass.ds(q * FT + t, 1)], xt,
                                                        ALU.mult, ALU.add)
                    last.then_inc(done_, 1)

            with dve.Fori(0, FC // YS) as r:
                for k in range(YS):
                    finish(r * YS + k, k, r * 32 + 32)


_INS = ["x", "adj", "L0_gnn_W", "L0_gnn_a", "L0_ffn_Wg", "L0_ffn_bg", "L0_ffn_W1", "L0_ffn_b1", "L0_ffn_W2",
        "L0_ffn_b2"]


def kernel(**inputs):
    import numpy as _np
    import concourse.bacc as _bacc
    from concourse import mybir as _mybir
    from concourse.bass_utils import run_bass_kernel_spmd as _run

    nc = _bacc.Bacc("TRN2", target_bir_lowering=False, num_devices=1)
    arrays, args = {}, []
    for name in _INS:
        v = _np.ascontiguousarray(inputs[name])
        arrays[f"in_{name}_dram"] = v
        args.append(nc.dram_tensor(f"in_{name}_dram", v.shape, _mybir.dt.from_np(v.dtype), kind="ExternalInput").ap())
    shape = inputs["x"].shape
    args.append(nc.dram_tensor("out_0_dram", shape, _mybir.dt.float32, kind="ExternalOutput").ap())
    graph_moe(nc, *args)
    r = _run(nc, [arrays], core_ids=[0])
    return r.results[0]["out_0_dram"]
```
